# Optimizing a Trainium2 kernel written in Bass

```python
import numpy as np
import jax
import jax.numpy as jnp

def _softmax(x, axis=-1):
    return jax.nn.softmax(x, axis=axis)
def _gelu(x):
    return jax.nn.gelu(x, approximate=True)
def _silu(x):
    return jax.nn.silu(x)
def _sigmoid(x):
    return jax.nn.sigmoid(x)
def _layernorm(x, axis=-1, eps=1e-5):
    m = jnp.mean(x, axis=axis, keepdims=True)
    v = jnp.var(x, axis=axis, keepdims=True)
    return (x - m) / jnp.sqrt(v + eps)
def _scatter_add(tgt, idx, src, axis=0):
    return tgt.at[idx].add(src)
def _segment_sum(src, seg, n):
    return jax.ops.segment_sum(src, seg, n)

kernel_name = 'mk_adj_resnorm_d2_adj_128_a2e952'

def setup_inputs(seed: int = 0):
    np.random.seed(seed)
    _w = jnp.asarray
    def _rec_inputs():
        import jax
        import jax.numpy as jnp
        _gk = jax.random.key(seed)
        x = -0.000929 + 1 * jax.random.normal(jax.random.fold_in(_gk, 1), (8192, 128), jnp.float32)
        _a = jax.random.bernoulli(jax.random.fold_in(_gk, 2), 0.000976562, (8192, 8192))
        _af = _a.astype(jnp.float32)
        adj = _af
        return x, adj
    x, adj = _rec_inputs()
    def _L0_gnn_setup():
        import jax, jax.numpy as jnp
        import numpy as np
        N, EMB, HID = (8192, 128, 128)
        key = jax.random.key(seed)
        k1, k2, k3, k4, k5, k6, k7, k8 = jax.random.split(key, 8)
        inlayer = jax.random.normal(k1, (N, EMB), dtype=jnp.float32)
        inlayer2 = jax.random.normal(k2, (N, 2 * EMB), dtype=jnp.float32)
        adj_mat = jax.random.randint(k3, (N, N), 0, 2).astype(jnp.float32)
        W1 = jax.random.normal(k4, (HID, 2 * EMB), dtype=jnp.float32) / np.sqrt(2 * EMB)
        w2 = jax.random.normal(k5, (HID,), dtype=jnp.float32) / np.sqrt(HID)
        b2 = jax.random.normal(k6, (), dtype=jnp.float32) * 0.01
        w3 = jax.random.normal(k7, (HID,), dtype=jnp.float32) / np.sqrt(HID)
        b3 = jax.random.normal(k8, (), dtype=jnp.float32) * 0.01
        return {'inlayer': inlayer, 'inlayer2': inlayer2, 'adj_mat': adj_mat, 'W1': W1, 'w2': w2, 'b2': b2, 'w3': w3, 'b3': b3}
    _L0_gnn_all = _L0_gnn_setup()
    _L0_gnn_in = {k: v for k, v in _L0_gnn_all.items() if k in ('inlayer2', 'W1', 'w2', 'b2', 'w3', 'b3', )}
    del _L0_gnn_all

    def _L1_gnn_setup():
        import jax, jax.numpy as jnp
        import numpy as np
        V0, V1, C = (64, 128, 128)
        V = V0 * V1
        key = jax.random.key(seed)
        ks = jax.random.split(key, 8)
        x = jax.random.normal(ks[0], (V, C), dtype=jnp.float32)
        edge_index = jax.random.randint(ks[1], (2, 100), 0, V)
        L = jnp.zeros((2, 2), dtype=jnp.float32)
        mass = jax.random.uniform(ks[2], (V,), dtype=jnp.float32) + 0.5
        evals0 = jax.random.uniform(ks[3], (V0,), dtype=jnp.float32) * 2.0
        evals1 = jax.random.uniform(ks[4], (V1,), dtype=jnp.float32) * 2.0
        evecs = jax.random.normal(ks[5], (V, V), dtype=jnp.float32) / np.float32(np.sqrt(V))
        diffusion_time = jax.random.uniform(ks[6], (2, C), dtype=jnp.float32)
        return {'x': x, 'edge_index': edge_index, 'L': L, 'mass': mass, 'evals0': evals0, 'evals1': evals1, 'evecs': evecs, 'diffusion_time': diffusion_time}
    _L1_gnn_all = _L1_gnn_setup()
    _L1_gnn_in = {k: v for k, v in _L1_gnn_all.items() if k in ('edge_index', 'L', 'mass', 'evals0', 'evals1', 'diffusion_time', )}
    del _L1_gnn_all

    return {
        "x": x,
        "adj": adj,
        "L0_gnn_inlayer2": _L0_gnn_in["inlayer2"],
        "L0_gnn_W1": _L0_gnn_in["W1"],
        "L0_gnn_w2": _L0_gnn_in["w2"],
        "L0_gnn_b2": _L0_gnn_in["b2"],
        "L0_gnn_w3": _L0_gnn_in["w3"],
        "L0_gnn_b3": _L0_gnn_in["b3"],
        "L1_gnn_edge_index": _L1_gnn_in["edge_index"],
        "L1_gnn_L": _L1_gnn_in["L"],
        "L1_gnn_mass": _L1_gnn_in["mass"],
        "L1_gnn_evals0": _L1_gnn_in["evals0"],
        "L1_gnn_evals1": _L1_gnn_in["evals1"],
        "L1_gnn_diffusion_time": _L1_gnn_in["diffusion_time"],
    }

def reference(x, adj, L0_gnn_inlayer2, L0_gnn_W1, L0_gnn_w2, L0_gnn_b2, L0_gnn_w3, L0_gnn_b3, L1_gnn_edge_index, L1_gnn_L, L1_gnn_mass, L1_gnn_evals0, L1_gnn_evals1, L1_gnn_diffusion_time):
    import jax
    import jax.numpy as jnp
    def _L0_gnn_ref(inlayer, inlayer2, adj_mat, W1, w2, b2, w3, b3):
        import jax, jax.numpy as jnp
        import numpy as np
        N, EMB, HID = (8192, 128, 128)
        in_fts = jnp.einsum('ne,he->nh', inlayer2, W1)
        f1 = in_fts @ w2 + b2
        f2 = in_fts @ w3 + b3
        logits = f1[:, None] + f2[None, :]
        logits = adj_mat * logits
        bias_mat = -1000000000.0 * (1.0 - (adj_mat > 0).astype(jnp.float32))
        coefs = jax.nn.softmax(jax.nn.leaky_relu(logits, 0.01) + bias_mat, axis=1)
        vals = coefs @ inlayer
        return vals

    def _L1_gnn_ref(x, edge_index, L, mass, evals0, evals1, evecs, diffusion_time):
        import jax, jax.numpy as jnp
        import numpy as np
        V0, V1, C = (64, 128, 128)
        V = V0 * V1
        x_spec = evecs.T @ (x * mass[:, None])
        e0 = jnp.exp(-evals0[:, None] * diffusion_time[0][None, :])
        e1 = jnp.exp(-evals1[:, None] * diffusion_time[1][None, :])
        diffusion_coefs = (e0[:, None, :] * e1[None, :, :]).reshape(V0 * V1, C)
        x_diffuse = evecs @ (diffusion_coefs * x_spec)
        return x_diffuse

    x = _layernorm(x + _L0_gnn_ref(x, L0_gnn_inlayer2, adj, L0_gnn_W1, L0_gnn_w2, L0_gnn_b2, L0_gnn_w3, L0_gnn_b3), axis=-1)
    x = _layernorm(x + _L1_gnn_ref(x, L1_gnn_edge_index, L1_gnn_L, L1_gnn_mass, L1_gnn_evals0, L1_gnn_evals1, adj, L1_gnn_diffusion_time), axis=-1)
    return x


_drawn_inputs = setup_inputs


def setup_inputs(seed=0):
    import zlib

    import numpy as np

    out = dict(_drawn_inputs(seed))
    spreads = {'L1_gnn_L': (0.0, 0.1)}
    factors = {}
    for name, (base, spread) in spreads.items():
        noise = np.random.default_rng([zlib.crc32(name.encode()), seed]).standard_normal(out[name].shape)
        drawn = base * np.exp(spread * noise) if base else spread * noise
        out[name] = jnp.asarray(drawn.astype(out[name].dtype))
    for name, factor in factors.items():
        out[name] = (out[name] * factor).astype(out[name].dtype)
    return out
```

```python
import concourse.bass as bass
from concourse import mybir
from contextlib import ExitStack

P = 128


def build(nc, adj, x, in2T, W1, w23, b23, mass_t, evals0, evals1, dt_rows, out):
    fp32, bf16, fp16 = mybir.dt.float32, mybir.dt.bfloat16, mybir.dt.float16
    fp8, u8 = mybir.dt.float8e4, mybir.dt.uint8
    ALU, ACT, AX = mybir.AluOpType, mybir.ActivationFunctionType, mybir.AxisListType

    N, C = x.shape
    EMB2 = in2T.shape[0]
    KE = EMB2 // P
    T = N // P
    BT = 8
    BW = BT * P
    NB = T // BT
    CB = 2
    CW = CB * BW
    NCH = N // CW
    HB = NB // 2
    Z = 2 * (C + 1)
    ZL = C + 1
    LO = 2.0 ** 11
    ZS = 2.0 ** 6
    YS = 2.0 ** 8
    GS = 2.0 ** -2
    EPS = 1e-5
    SLOPE = 0.01
    G = NB
    PI = 8
    NPC = T // PI
    RING = 4

    adjT8 = nc.dram_tensor("adjT8", (T, P, T * P), u8, kind="Internal").ap()
    adj8 = nc.dram_tensor("adj8", (G, P, T, BW), u8, kind="Internal").ap()
    x1_d = nc.dram_tensor("x1_d", (T, P, C), fp32, kind="Internal").ap()
    x_t = x.rearrange("(t p) c -> t p c", p=P)
    out_t = out.rearrange("(t p) c -> t p c", p=P)
    adj_t = adj.rearrange("(t p) j -> t p j", p=P)

    ctx = ExitStack()
    with ctx:
        def sb(name, shape, dt):
            return ctx.enter_context(nc.sbuf_tensor(name, shape, dt))

        def sem(name):
            return ctx.enter_context(nc.semaphore(name))

        f2_region = sb("f2_region", [P, N * 4], u8)
        f2row = f2_region[:, :].bitcast(fp32)
        piece = f2_region[:, :].bitcast(fp8).rearrange("p (r t j) -> p r t j", r=RING, t=PI)
        piece_b = f2_region[:, :].rearrange("p (r t j) -> p r t j", r=RING, t=PI)
        z_region = sb("z_region", [P, T * 2 * Z * 2], u8)
        z = z_region[:, :].bitcast(fp16).rearrange("p (t m c) -> p t m c", m=2, c=Z)
        in2 = z_region[:, 0:KE * N * 4].bitcast(fp32).rearrange("p (k n) -> p k n", k=KE)
        z2 = z_region[:, 0:T * 2 * C * 2].bitcast(fp16).rearrange("p (t c) -> p t c", t=T)
        slab_b = z_region[:, N * 4:N * 4 + RING * N].rearrange("p (r j) -> p r j", r=RING)
        slab = z_region[:, N * 4:N * 4 + RING * N].bitcast(fp8).rearrange("p (r j) -> p r j", r=RING)
        y_region = sb("y_region", [P, T * 2 * C * 2], u8)
        y = y_region[:, :].bitcast(fp16).rearrange("p (t c) -> p t c", t=T)
        x_all = y_region[:, :].bitcast(fp32).rearrange("p (t c) -> p t c", t=T)
        a_ring = sb("a_ring", [P, NCH, CW], bf16)
        wide = sb("wide", [P, 3, CW], bf16)
        spos = wide[:, 0, :]
        labels = wide[:, 1:3, :]
        wide_f = [wide[:, k, :].bitcast(fp32).rearrange("p (t c) -> p t c", t=BT) for k in range(3)]
        labT = sb("labT", [P, 2, BW], bf16)
        m_pos = sb("m_pos", [P, 2, BW], bf16)
        m_neg = sb("m_neg", [P, 2, BW], bf16)
        aT_half = sb("aT_half", [P, 2, HB * BW], u8)
        aN_half = sb("aN_half", [P, 2, HB * BW], u8)
        ident = sb("ident", [P, P], bf16)
        inv_n = sb("inv_n", [P, P], fp32)
        w1s = sb("w1s", [P, EMB2], fp32)
        w23s = sb("w23s", [P, 2], fp32)
        b23s = sb("b23s", [P, 2], fp32)
        v23 = sb("v23", [P, KE, 2], fp32)
        v3rep = sb("v3rep", [P, KE, P], fp32)
        f1 = sb("f1", [P, T], fp32)
        nf1 = sb("nf1", [P, T], fp32)
        f2 = sb("f2", [P, T], fp32)
        top = sb("top", [P, 4], fp32)
        F2 = sb("F2", [P, 1], fp32)
        tmp_a = sb("tmp_a", [P, T], fp32)
        tmp_b = sb("tmp_b", [P, T], fp32)
        row_pos = sb("row_pos", [P, 2, T], fp32)
        row_neg = sb("row_neg", [P, 2, T], fp32)
        wj = sb("wj", [P, 2, T], fp32)
        mass = sb("mass", [P, T], fp32)
        xmean = sb("xmean", [P, C], fp32)
        eps = sb("eps", [P, 1], fp32)
        ev0 = sb("ev0", [P, T], fp32)
        ev1 = sb("ev1", [P, 1], fp32)
        dts = sb("dts", [P, 2, C], fp32)
        e1 = sb("e1", [P, C], fp32)
        xt = sb("xt", [P, 2, C], fp32)
        u = sb("u", [P, ZL], fp32)
        col = sb("col", [P, 4], fp32)
        tt = sb("tt", [P, C], fp32)
        st = sb("st", [P, 6], fp32)
        mv = sb("mv", [P, 2], fp32)
        sd = sb("sd", [P, 1], fp32)
        x1 = sb("x1", [P, 2, C], fp32)
        ym = sb("ym", [P, C], fp32)

        bank = [ctx.enter_context(nc.psum_tensor(f"bank{k}", [P, 512], fp32)) for k in range(8)]
        tp = [bank[4 + k][:, :].bitcast(bf16) for k in range(4)]

        def acc(ib_par, m):
            return bank[2 * ib_par + m][:, 0:Z]

        weights_loaded, consts_loaded, in2_loaded, x_loaded = map(sem, (
            "weights_loaded", "consts_loaded", "in2_loaded", "x_loaded"))
        ident_step, ones_ready = sem("ident_step"), sem("ones_ready")
        v_summed, v_ready, fcol_summed, frow_summed, frow_ready, mean_summed, mean_ready = map(sem, (
            "v_summed", "v_ready", "fcol_summed", "frow_summed", "frow_ready", "mean_summed", "mean_ready"))
        dve_prep, act_prep = sem("dve_prep"), sem("act_prep")
        zt_ready, zhi_ready, zd_ready, zlo_ready = map(sem, ("zt_ready", "zhi_ready", "zd_ready", "zlo_ready"))
        adj_loaded = [sem(f"adj_loaded{k}") for k in range(NCH)]
        spos_ready, labels_ready, transposed, labT_ready, aT_ready, masks_ready, multiplied = map(sem, (
            "spos_ready", "labels_ready", "transposed", "labT_ready", "aT_ready", "masks_ready", "multiplied"))
        aN_ready = sem("aN_ready")
        aT_stored = [sem(f"aT_stored{k}") for k in range(2)]
        aN_stored = [sem(f"aN_stored{k}") for k in range(2)]
        xt_loaded = [sem(f"xt_loaded{k}") for k in range(2)]
        x1_stored = [sem(f"x1_stored{k}") for k in range(2)]
        fin, sd_ready, y_step = sem("fin"), sem("sd_ready"), sem("y_step")
        piece_loaded = [sem(f"piece_loaded{k}") for k in range(RING)]
        piece_used = sem("piece_used")
        lo_ready, spec_step, e_arg_ready, e_ready, zh2_ready, z2_ready = map(sem, (
            "lo_ready", "spec_step", "e_arg_ready", "e_ready", "zh2_ready", "z2_ready"))
        slab_loaded = [sem(f"slab_loaded{k}") for k in range(RING)]
        rows_done, lo3_ready, fin3, sd3_ready = map(sem, ("rows_done", "lo3_ready", "fin3", "sd3_ready"))
        xr_loaded = [sem(f"xr_loaded{k}") for k in range(2)]
        out_stored = [sem(f"out_stored{k}") for k in range(2)]

        FIN = 13
        FIN3 = 6
        SPEC = 4
        YST = 3

        block = ctx.enter_context(nc.Block())

        def ab(t, shape):
            return t.to_broadcast(shape)

        waits_passed = {n: sem(f"waits_passed_{n}") for n in ("sp", "pool", "dve", "pe")}

        def passed(eng, name):
            eng.sem_inc(waits_passed[name], 1)

        @block.sync
        def _(sp):
            sp.dma_start(w1s[:, :], W1).then_inc(weights_loaded, 16)
            sp.dma_start(w23s[:, :], w23).then_inc(weights_loaded, 16)
            sp.dma_start(b23s[:, :], b23.partition_broadcast(P)).then_inc(weights_loaded, 16)
            sp.dma_start(in2, in2T.rearrange("(k p) n -> p k n", p=P)).then_inc(in2_loaded, 16)
            sp.dma_start(x_all, x.rearrange("(t p) c -> p t c", p=P)).then_inc(x_loaded, 16)
            sp.dma_start(mass[:, :], mass_t).then_inc(consts_loaded, 16)
            sp.dma_start(ev0[:, :], evals0.partition_broadcast(P)).then_inc(consts_loaded, 16)
            sp.dma_start(ev1[:, :], evals1).then_inc(consts_loaded, 16)
            sp.dma_start(dts[:, :, :], dt_rows.partition_broadcast(P)).then_inc(consts_loaded, 16)

            def x1_store(ib, par):
                sp.wait_ge(fin, FIN * ib + FIN)
                passed(sp, "sp")
                sp.dma_start(x1_d[ib], x1[:, par, :]).then_inc(x1_stored[par], 16)

            def row_block(ib, par, first):
                if not first:
                    sp.wait_ge(fin, FIN * (ib - 2) + 9)
                passed(sp, "sp")
                sp.dma_start(xt[:, par, :], x_t[ib]).then_inc(xt_loaded[par], 16)
                for h in range(2):
                    sp.wait_ge(aN_ready, NCH * ib + NCH // 2 * (h + 1))
                    passed(sp, "sp")
                    sp.dma_start(adj8[h * HB:(h + 1) * HB, :, ib].rearrange("g p j -> p g j"),
                                 aN_half[:, h, :].rearrange("p (g j) -> p g j", g=HB)
                                 ).then_inc(aN_stored[h], 16)
                    sp.wait_ge(aT_ready, NB * ib + HB * (h + 1))
                    passed(sp, "sp")
                    sp.dma_start(adjT8[ib, :, h * HB * BW:(h + 1) * HB * BW],
                                 aT_half[:, h, :]).then_inc(aT_stored[h], 16)
                    if h == 0 and not (first and par == 0):
                        x1_store(ib - 1, 1 - par)

            row_block(0, 0, True)
            row_block(1, 1, True)
            with sp.Fori(1, T // 2) as q:
                for par in range(2):
                    row_block(2 * q + par, par, False)
            x1_store(T - 1, 1)

            for h in range(2):
                sp.wait_ge(aN_stored[h], 16 * T)
            sp.wait_ge(spos_ready, NCH * T)

            def load_piece(g, k, reuse):
                if reuse:
                    sp.wait_ge(piece_used, NPC * g + k - RING + 1)
                passed(sp, "sp")
                sp.dma_start(piece_b[:, k % RING], adj8[g, :, k * PI:(k + 1) * PI, :]
                             ).then_inc(piece_loaded[k % RING], 16)

            for k in range(NPC):
                load_piece(0, k, k >= RING)
            with sp.Fori(1, G) as g:
                for k in range(NPC):
                    load_piece(g, k, True)

            for h in range(2):
                sp.wait_ge(aT_stored[h], 16 * T)
                sp.wait_ge(x1_stored[h], 16 * (T // 2))
            sp.wait_ge(multiplied, NB * T)

            def out_store(ib, par):
                sp.wait_ge(fin3, FIN3 * ib + FIN3)
                passed(sp, "sp")
                sp.dma_start(out_t[ib], x1[:, par, :]).then_inc(out_stored[par], 16)

            def load_slab(ib, k, first):
                if not first:
                    sp.wait_ge(rows_done, ib - RING + 1)
                passed(sp, "sp")
                sp.dma_start(slab_b[:, k, :], adjT8[ib]).then_inc(slab_loaded[k], 16)

            def load_x1(ib, par, first):
                if not first:
                    sp.wait_ge(fin3, FIN3 * (ib - 2) + 2)
                passed(sp, "sp")
                sp.dma_start(xt[:, par, :], x1_d[ib]).then_inc(xr_loaded[par], 16)

            sp.wait_ge(fin, FIN * T)
            for k in range(RING):
                load_slab(k, k, True)
            for k in range(2):
                load_x1(k, k, True)
            with sp.Fori(0, T // RING - 1) as q:
                for k in range(RING):
                    ib = RING * q + k
                    out_store(ib, k % 2)
                    load_x1(ib + 2, k % 2, False)
                    load_slab(ib + RING, k, False)
            for k in range(RING):
                ib = T - RING + k
                out_store(ib, k % 2)
                if k < 2:
                    load_x1(ib + 2, k % 2, False)
            for par in range(2):
                sp.wait_ge(out_stored[par], 16 * (T // 2))

        @block.gpsimd
        def _(pool):
            pool.memset(ident[:, :], 0.0).then_inc(ident_step, 1)
            pool.memset(inv_n[:, :], 1.0 / N).then_inc(ones_ready, 1)
            pool.memset(eps[:, :], EPS).then_inc(ones_ready, 1)
            pool.wait_ge(ident_step, 1)
            pool.affine_select(out=ident[:, :], in_=ident[:, :], compare_op=ALU.not_equal, fill=1.0,
                               base=0, pattern=[[-1, P]], channel_multiplier=1).then_inc(ident_step, 1)

            def load(ib, c):
                pool.dma_start(a_ring[:, c, :], adj_t[ib, :, c * CW:(c + 1) * CW]).then_inc(adj_loaded[c], 16)

            def pack(ib, c, reuse):
                pool.wait_ge(adj_loaded[c], 16 * ib + 16)
                if reuse and c % 2 == 0:
                    pool.wait_ge(aN_stored[c // 2], 16 * ib)
                passed(pool, "pool")
                dst = aN_half[:, c // 2, (c % 2) * CW:(c % 2 + 1) * CW].bitcast(fp8)
                pool.tensor_copy(dst, a_ring[:, c, :], saturate=False).then_inc(aN_ready, 1)

            def reload(ib, c):
                pool.wait_ge(aN_ready, NCH * ib + c + 1)
                pool.wait_ge(labels_ready, NCH * ib + c + 1)
                load(ib + 1, c)

            def y_of(ib, par, first=False):
                if not first:
                    pool.wait_ge(y_step, YST * ib)
                pool.wait_ge(fin, FIN * ib + FIN)
                pool.tensor_tensor(ym[:, :], x1[:, par, :], ab(mass[:, bass.ds(ib, 1)], [P, C]), ALU.mult
                                   ).then_inc(y_step, 1)
                pool.wait_ge(y_step, YST * ib + 1)
                pool.tensor_copy(y[:, ib, 0:C], ym[:, :]
                                 ).then_inc(y_step, 1)
                pool.wait_ge(y_step, YST * ib + 2)
                pool.tensor_tensor(y[:, ib, C:2 * C], ym[:, :], y[:, ib, 0:C], ALU.subtract
                                   ).then_inc(y_step, 1)

            def row_block(ib, par, first, last):
                for c in range(NCH):
                    pack(ib, c, not (first and par == 0))
                    if not last:
                        reload(ib, c)
                    if c == 2 and not (first and par == 0):
                        y_of(ib - 1, 1 - par, first)

            for c in range(NCH):
                load(0, c)
            pool.wait_ge(consts_loaded, 64)
            pool.wait_ge(zlo_ready, 2 * NB)
            pool.wait_ge(mean_ready, 1)
            row_block(0, 0, True, False)
            row_block(1, 1, True, False)
            with pool.Fori(1, T // 2 - 1) as q:
                for par in range(2):
                    row_block(2 * q + par, par, False, False)
            row_block(T - 2, 0, False, False)
            row_block(T - 1, 1, False, True)
            y_of(T - 1, 1)

        @block.scalar
        def _(act):
            act.wait_ge(weights_loaded, 48)
            for s in range(N // 512):
                act.wait_ge(frow_summed, s + 1)
                act.activation(f2row[:, s * 512:(s + 1) * 512], bank[4 + s % 4][:, :], ACT.Identity,
                               bias=b23s[:, 1:2]).then_inc(frow_ready, 1)
            act.wait_ge(dve_prep, 10)
            act.activation(row_pos[:, 0, :], tmp_a[:, :], ACT.Exp, scale=1.0 - SLOPE).then_inc(act_prep, 1)
            act.activation(row_neg[:, 0, :], tmp_b[:, :], ACT.Exp, scale=SLOPE - 1.0).then_inc(act_prep, 1)
            act.activation(wj[:, 0, :], f2[:, :], ACT.Exp).then_inc(act_prep, 1)
            act.activation(wj[:, 1, :], f2[:, :], ACT.Exp, scale=SLOPE).then_inc(act_prep, 1)
            act.wait_ge(consts_loaded, 64)
            act.wait_ge(dve_prep, 12)
            act.activation(e1[:, :], e1[:, :], ACT.Exp, scale=-1.0).then_inc(act_prep, 1)
            for n in range(2 * NB):
                m, h = n % 2, n // 2
                act.wait_ge(zt_ready, n + 1)
                act.activation(z[:, h * BT:(h + 1) * BT, m, 0:C], wide_f[m], ACT.Copy).then_inc(zhi_ready, 1)
                act.wait_ge(zd_ready, n + 1)
                act.activation(z[:, h * BT:(h + 1) * BT, m, ZL:ZL + C], wide_f[m], ACT.Copy, scale=LO
                               ).then_inc(zlo_ready, 1)

            def bank_out(ib, b, first):
                n = NB * ib + b
                act.wait_ge(transposed, n + 1)
                if not (first and b < 2):
                    act.wait_ge(masks_ready, n - 1)
                if not first and b % HB == 0:
                    act.wait_ge(aT_stored[b // HB], 16 * ib)
                act.activation(labT[:, b % 2, :], tp[b % 4], ACT.Copy).then_inc(labT_ready, 1)
                dst = aT_half[:, b // HB, (b % HB) * BW:(b % HB + 1) * BW].bitcast(fp8)
                act.activation(dst, tp[b % 4], ACT.Sign, saturate=False).then_inc(aT_ready, 1)

            def deviation(ib):
                act.wait_ge(fin, FIN * ib + 11)
                act.activation(sd[:, :], mv[:, 1:2], ACT.Sqrt, bias=eps[:, :]).then_inc(sd_ready, 1)

            def row_block(ib, first):
                for b in range(NB):
                    bank_out(ib, b, first)
                    if b == 2 and not first:
                        deviation(ib - 1)

            act.wait_ge(ones_ready, 2)
            row_block(0, True)
            with act.Fori(1, T) as ib:
                row_block(ib, False)
            deviation(T - 1)

            def group(g, par, first):
                act.wait_ge(piece_used, NPC * g + NPC)
                if not first:
                    act.wait_ge(spec_step, SPEC * g)
                for k in range(4):
                    act.activation(wide_f[0][:, 2 * k:2 * k + 2, :],
                                   bank[4 * par + k][:, :].rearrange("p (t c) -> p t c", t=2)[:, :, C:2 * C],
                                   ACT.Copy, scale=1.0 / (LO * YS)).then_inc(lo_ready, 1)
                act.wait_ge(e_arg_ready, g + 1)
                act.activation(wide_f[1], wide_f[1], ACT.Exp, scale=-1.0).then_inc(e_ready, 1)
                act.wait_ge(spec_step, SPEC * g + 3)
                act.activation(z2[:, bass.ds(g * BT, BT), 0:C], wide_f[0], ACT.Copy, scale=GS
                               ).then_inc(zh2_ready, 1)
                act.wait_ge(spec_step, SPEC * g + 4)
                act.activation(z2[:, bass.ds(g * BT, BT), C:2 * C], wide_f[2], ACT.Copy, scale=LO
                               ).then_inc(z2_ready, 1)

            for par in range(2):
                group(par, par, par == 0)
            with act.Fori(1, G // 2) as q:
                for par in range(2):
                    group(2 * q + par, par, False)

            def finish(ib, k):
                act.wait_ge(rows_done, ib + 1)
                act.activation(u[:, 0:C], bank[k][:, C:2 * C], ACT.Copy, scale=1.0 / (LO * GS)
                               ).then_inc(lo3_ready, 1)
                act.wait_ge(fin3, FIN3 * ib + 4)
                act.activation(sd[:, :], mv[:, 1:2], ACT.Sqrt, bias=eps[:, :]).then_inc(sd3_ready, 1)

            for k in range(RING):
                finish(k, k)
            with act.Fori(1, T // RING) as q:
                for k in range(RING):
                    finish(RING * q + k, k)

        @block.vector
        def _(dve):
            dve.wait_ge(v_summed, 1)
            dve.tensor_copy(v23[:, :, :], bank[1][:, 0:2 * KE].rearrange("p (k w) -> p k w", k=KE)
                            ).then_inc(v_ready, 1)
            for k in range(KE):
                dve.tensor_copy(v3rep[:, k, :], ab(bank[1][:, 2 * k + 1:2 * k + 2], [P, P])).then_inc(v_ready, 1)
            dve.wait_ge(weights_loaded, 48)
            dve.wait_ge(fcol_summed, 1)
            fc = bank[0][:, 0:2 * T].rearrange("p (t w) -> p t w", w=2)
            dve.tensor_scalar(f1[:, :], fc[:, :, 0], b23s[:, 0:1], None, ALU.add).then_inc(dve_prep, 1)
            dve.tensor_scalar(f2[:, :], fc[:, :, 1], b23s[:, 1:2], None, ALU.add).then_inc(dve_prep, 1)
            for k in range(4):
                dve.wait_ge(frow_ready, 4 * k + 4)
                dve.reduce_max(top[:, k:k + 1], f2row[:, k * 2048:(k + 1) * 2048], axis=AX.X).then_inc(dve_prep, 1)
            dve.wait_ge(dve_prep, 6)
            dve.reduce_max(F2[:, :], top[:, :], axis=AX.X).then_inc(dve_prep, 1)
            dve.wait_ge(dve_prep, 7)
            dve.tensor_scalar(tmp_a[:, :], f1[:, :], F2[:, :], 0.0, ALU.add, ALU.min).then_inc(dve_prep, 1)
            dve.tensor_scalar(tmp_b[:, :], f1[:, :], F2[:, :], 0.0, ALU.add, ALU.max).then_inc(dve_prep, 1)
            dve.tensor_scalar(f2[:, :], f2[:, :], F2[:, :], None, ALU.subtract).then_inc(dve_prep, 1)
            dve.tensor_scalar(nf1[:, :], f1[:, :], -1.0, None, ALU.mult).then_inc(dve_prep, 1)
            dve.wait_ge(consts_loaded, 64)
            dve.tensor_scalar(e1[:, :], dts[:, 1, :], ev1[:, :], None, ALU.mult).then_inc(dve_prep, 1)
            dve.tensor_scalar(mass[:, :], mass[:, :], YS, None, ALU.mult).then_inc(dve_prep, 1)
            dve.wait_ge(mean_summed, 1)
            dve.tensor_copy(xmean[:, :], bank[2][:, 0:C]).then_inc(mean_ready, 1)
            dve.wait_ge(act_prep, 4)
            for r in (row_pos, row_neg):
                dve.tensor_scalar(r[:, 1, :], r[:, 0, :], 1.0 / (ZS * LO), None, ALU.mult).then_inc(dve_prep, 1)
            dve.tensor_scalar(wj[:, :, :], wj[:, :, :], ZS, None, ALU.mult).then_inc(dve_prep, 1)
            dve.wait_ge(dve_prep, 16)
            for r in (row_pos, row_neg):
                dve.tensor_scalar(r[:, 0, :], r[:, 0, :], 1.0 / ZS, None, ALU.mult).then_inc(dve_prep, 1)
            for m in range(2):
                dve.tensor_copy(z[:, :, m, C], wj[:, m, :]).then_inc(dve_prep, 1)
            dve.wait_ge(dve_prep, 20)
            for m, d in enumerate((tmp_a, tmp_b)):
                dve.tensor_tensor(d[:, :], wj[:, m, :], z[:, :, m, C], ALU.subtract).then_inc(dve_prep, 1)
            dve.wait_ge(dve_prep, 22)
            for m, d in enumerate((tmp_a, tmp_b)):
                dve.tensor_scalar(z[:, :, m, C + ZL], d[:, :], LO, None, ALU.mult).then_inc(dve_prep, 1)
            dve.wait_ge(x_loaded, 16)

            def table_product(n):
                m, h = n % 2, n // 2
                if n >= 2:
                    dve.wait_ge(zlo_ready, n - 1)
                dve.tensor_tensor(wide_f[m], x_all[:, h * BT:(h + 1) * BT, :],
                                  wj[:, m, h * BT:(h + 1) * BT].unsqueeze(2).to_broadcast([P, BT, C]),
                                  ALU.mult).then_inc(zt_ready, 1)

            def table_rest(n):
                m, h = n % 2, n // 2
                dve.wait_ge(zhi_ready, n + 1)
                dve.tensor_tensor(wide_f[m], wide_f[m], z[:, h * BT:(h + 1) * BT, m, 0:C], ALU.subtract
                                  ).then_inc(zd_ready, 1)

            table_product(0)
            for n in range(2 * NB):
                if n + 1 < 2 * NB:
                    table_product(n + 1)
                table_rest(n)
            dve.wait_ge(zlo_ready, 2 * NB)

            def label(ib, c, fresh):
                n = NCH * ib + c
                if not (fresh and c == 0):
                    dve.wait_ge(labels_ready, n)
                dve.tensor_scalar(spos, f2row[:, c * CW:(c + 1) * CW], nf1[:, bass.ds(ib, 1)], 1.0,
                                  ALU.is_gt, ALU.add).then_inc(spos_ready, 1)
                dve.wait_ge(spos_ready, n + 1)
                dve.wait_ge(adj_loaded[c], 16 * ib + 16)
                if not (fresh and c < 2):
                    dve.wait_ge(transposed, 2 * n - 2)
                dve.tensor_tensor(labels[:, c % 2, :], spos, a_ring[:, c, :], ALU.mult).then_inc(labels_ready, 1)

            def masks(ib, b, fresh):
                n = NB * ib + b
                dve.wait_ge(labT_ready, n + 1)
                if not (fresh and b < 2):
                    dve.wait_ge(multiplied, n - 1)
                dve.tensor_scalar(m_pos[:, b % 2, :], labT[:, b % 2, :], 2.0, None, ALU.is_equal)
                dve.tensor_scalar(m_neg[:, b % 2, :], labT[:, b % 2, :], 1.0, None, ALU.is_equal
                                  ).then_inc(masks_ready, 1)

            def attend(ib, par):
                n = FIN * ib
                pos, neg = acc(par, 0), acc(par, 1)
                one = bass.ds(ib, 1)
                dve.wait_ge(multiplied, NB * ib + NB)
                dve.tensor_scalar(u[:, :], pos[:, 0:ZL], row_pos[:, 0, one], None, ALU.mult).then_inc(fin, 1)
                dve.wait_ge(fin, n + 1)
                dve.scalar_tensor_tensor(u[:, :], pos[:, ZL:Z], row_pos[:, 1, one], u[:, :], ALU.mult, ALU.add
                                         ).then_inc(fin, 1)
                dve.wait_ge(fin, n + 2)
                dve.scalar_tensor_tensor(u[:, :], neg[:, 0:ZL], row_neg[:, 0, one], u[:, :], ALU.mult, ALU.add
                                         ).then_inc(fin, 1)
                dve.wait_ge(fin, n + 3)
                dve.scalar_tensor_tensor(u[:, :], neg[:, ZL:Z], row_neg[:, 1, one], u[:, :], ALU.mult, ALU.add
                                         ).then_inc(fin, 1)
                dve.wait_ge(fin, n + 4)
                dve.tensor_scalar(col[:, 0:1], u[:, C:ZL], 0.0, None, ALU.is_le).then_inc(fin, 1)
                dve.wait_ge(fin, n + 5)
                dve.tensor_tensor(col[:, 1:2], u[:, C:ZL], col[:, 0:1], ALU.add).then_inc(fin, 1)
                dve.wait_ge(fin, n + 6)
                dve.reciprocal(col[:, 2:3], col[:, 1:2]).then_inc(fin, 1)
                dve.scalar_tensor_tensor(tt[:, :], xmean[:, :], col[:, 0:1], u[:, 0:C], ALU.mult, ALU.add
                                         ).then_inc(fin, 1)
                dve.wait_ge(fin, n + 8)
                dve.wait_ge(xt_loaded[par], 8 * (ib - par) + 16)
                dve.scalar_tensor_tensor(tt[:, :], tt[:, :], col[:, 2:3], xt[:, par, :], ALU.mult, ALU.add
                                         ).then_inc(fin, 1)
                dve.wait_ge(fin, n + 9)
                dve.bn_stats(st[:, :], tt[:, :]).then_inc(fin, 1)
                dve.wait_ge(fin, n + 10)
                passed(dve, "dve")
                dve.bn_aggr(mv[:, :], st[:, :]).then_inc(fin, 1)

            def normalize(ib, par, reuse):
                n = FIN * ib
                dve.wait_ge(sd_ready, ib + 1)
                dve.reciprocal(col[:, 3:4], sd[:, :]).then_inc(fin, 1)
                dve.wait_ge(fin, n + 12)
                if reuse:
                    dve.wait_ge(x1_stored[par], 8 * (ib - par))
                    dve.wait_ge(y_step, YST * ib - 2 * YST + 1)
                dve.tensor_scalar(x1[:, par, :], tt[:, :], mv[:, 0:1], col[:, 3:4], ALU.subtract, ALU.mult
                                  ).then_inc(fin, 1)

            def row_block(ib, par, fresh, last, tail, reuse):
                for b in range(NB):
                    masks(ib, b, fresh)
                    if tail and b == 1:
                        attend(ib - 1, 1 - par)
                    if tail and b == 2:
                        normalize(ib - 1, 1 - par, reuse)
                    if b % 2:
                        c = (b + 1) // 2 + 1
                        if c < NCH:
                            label(ib, c, fresh)
                        elif not last:
                            label(ib + 1, c - NCH, False)

            label(0, 0, True)
            label(0, 1, True)
            row_block(0, 0, True, False, False, False)
            row_block(1, 1, False, False, True, False)
            row_block(2, 0, False, False, True, False)
            row_block(3, 1, False, False, True, True)
            with dve.Fori(2, T // 2 - 1) as q:
                for par in range(2):
                    row_block(2 * q + par, par, False, False, True, True)
            row_block(T - 2, 0, False, False, True, True)
            row_block(T - 1, 1, False, True, True, True)
            attend(T - 1, 1)
            normalize(T - 1, 1, True)

            def spectrum(g, par, first):
                n = SPEC * g
                if not first:
                    dve.wait_ge(z2_ready, g)
                dve.tensor_tensor(wide_f[1], dts[:, 0, :].unsqueeze(1).to_broadcast([P, BT, C]),
                                  ev0[:, bass.ds(g * BT, BT)].unsqueeze(2).to_broadcast([P, BT, C]), ALU.mult
                                  ).then_inc(e_arg_ready, 1)
                for k in range(4):
                    dve.wait_ge(lo_ready, 4 * g + k + 1)
                    last = dve.scalar_tensor_tensor(
                        wide_f[0][:, 2 * k:2 * k + 2, :],
                        bank[4 * par + k][:, :].rearrange("p (t c) -> p t c", t=2)[:, :, 0:C], 1.0 / YS,
                        wide_f[0][:, 2 * k:2 * k + 2, :], ALU.mult, ALU.add)
                last.then_inc(spec_step, 1)
                dve.wait_ge(spec_step, n + 1)
                dve.tensor_tensor(wide_f[0], wide_f[0], e1[:, :].unsqueeze(1).to_broadcast([P, BT, C]), ALU.mult
                                  ).then_inc(spec_step, 1)
                dve.wait_ge(spec_step, n + 2)
                dve.wait_ge(e_ready, g + 1)
                dve.tensor_tensor(wide_f[0], wide_f[0], wide_f[1], ALU.mult).then_inc(spec_step, 1)
                dve.wait_ge(spec_step, n + 3)
                dve.wait_ge(zh2_ready, g + 1)
                dve.scalar_tensor_tensor(wide_f[2], wide_f[0], GS, z2[:, bass.ds(g * BT, BT), 0:C],
                                         ALU.mult, ALU.subtract).then_inc(spec_step, 1)

            dve.wait_ge(act_prep, 5)
            spectrum(0, 0, True)
            spectrum(1, 1, False)
            with dve.Fori(1, G // 2) as q:
                for par in range(2):
                    spectrum(2 * q + par, par, False)

            def rows(ib, k, first):
                n, par = FIN3 * ib, k % 2
                if not (first and k == 0):
                    dve.wait_ge(fin3, n)
                dve.wait_ge(lo3_ready, ib + 1)
                dve.scalar_tensor_tensor(tt[:, :], bank[k][:, 0:C], 1.0 / GS, u[:, 0:C], ALU.mult, ALU.add
                                         ).then_inc(fin3, 1)
                dve.wait_ge(fin3, n + 1)
                dve.wait_ge(xr_loaded[par], 8 * (ib - par) + 16)
                dve.tensor_tensor(tt[:, :], tt[:, :], xt[:, par, :], ALU.add).then_inc(fin3, 1)
                dve.wait_ge(fin3, n + 2)
                dve.bn_stats(st[:, :], tt[:, :]).then_inc(fin3, 1)
                dve.wait_ge(fin3, n + 3)
                passed(dve, "dve")
                dve.bn_aggr(mv[:, :], st[:, :]).then_inc(fin3, 1)
                dve.wait_ge(sd3_ready, ib + 1)
                dve.reciprocal(col[:, 3:4], sd[:, :]).then_inc(fin3, 1)
                dve.wait_ge(fin3, n + 5)
                if not (first and k < 2):
                    dve.wait_ge(out_stored[par], 8 * (ib - par))
                dve.tensor_scalar(x1[:, par, :], tt[:, :], mv[:, 0:1], col[:, 3:4], ALU.subtract, ALU.mult
                                  ).then_inc(fin3, 1)

            for par in range(2):
                dve.wait_ge(x1_stored[par], 16 * (T // 2))
            dve.wait_ge(y_step, YST * T)
            for k in range(RING):
                rows(k, k, True)
            with dve.Fori(1, T // RING) as q:
                for k in range(RING):
                    rows(RING * q + k, k, False)

        @block.tensor
        def _(pe):
            pe.wait_ge(weights_loaded, 48)
            for k in range(KE):
                last = pe.matmul(bank[1][:, 2 * k:2 * k + 2], w1s[:, k * P:(k + 1) * P], w23s[:, :],
                                 start=True, stop=True)
            last.then_inc(v_summed, 1)
            pe.wait_ge(v_ready, 1 + KE)
            pe.wait_ge(in2_loaded, 16)
            for s in range(N // 512):
                if s >= 4:
                    pe.wait_ge(frow_ready, s - 3)
                for k in range(KE):
                    last = pe.matmul(bank[4 + s % 4][:, :], v3rep[:, k, :], in2[:, k, s * 512:(s + 1) * 512],
                                     start=(k == 0), stop=(k == KE - 1))
                last.then_inc(frow_summed, 1)
            for t in range(T):
                for k in range(KE):
                    last = pe.matmul(bank[0][:, 2 * t:2 * t + 2], in2[:, k, t * P:(t + 1) * P], v23[:, k, :],
                                     start=(k == 0), stop=(k == KE - 1))
            last.then_inc(fcol_summed, 1)
            pe.wait_ge(x_loaded, 16)
            pe.wait_ge(ones_ready, 2)
            for t in range(T):
                last = pe.matmul(bank[2][:, 0:C], inv_n[:, :], x_all[:, t, :], start=(t == 0), stop=(t == T - 1))
            last.then_inc(mean_summed, 1)

            def transposes(ib, b, fresh):
                n = NB * ib + b
                if b % CB == 0:
                    pe.wait_ge(labels_ready, NCH * ib + b // CB + 1)
                if not (fresh and b < 4):
                    pe.wait_ge(aT_ready, n - 3)
                for k in range(BT):
                    at = (b % CB) * BW + k * P
                    last = pe.transpose(tp[b % 4][:, k * P:(k + 1) * P],
                                        labels[:, b // CB % 2, at:at + P], ident[:, :])
                last.then_inc(transposed, 1)

            def products(ib, b, par, reuse):
                n = NB * ib + b
                pe.wait_ge(masks_ready, n + 1)
                if reuse and b == 0:
                    pe.wait_ge(fin, FIN * ib - 2 * FIN + 4)
                for k in range(BT):
                    t = b * BT + k
                    for m, mask in enumerate((m_pos, m_neg)):
                        last = pe.matmul(acc(par, m), mask[:, b % 2, k * P:(k + 1) * P], z[:, t, m, :],
                                         start=(t == 0), stop=(t == T - 1))
                last.then_inc(multiplied, 1)

            def row_block(ib, par, fresh, last, reuse):
                for b in range(NB):
                    if b + 2 < NB:
                        transposes(ib, b + 2, fresh)
                    elif not last:
                        transposes(ib + 1, b + 2 - NB, False)
                    products(ib, b, par, reuse)

            pe.wait_ge(ident_step, 2)
            pe.wait_ge(frow_ready, N // 512)
            transposes(0, 0, True)
            transposes(0, 1, True)
            pe.wait_ge(mean_ready, 1)
            pe.wait_ge(dve_prep, 24)
            pe.wait_ge(zlo_ready, 2 * NB)
            row_block(0, 0, True, False, False)
            row_block(1, 1, False, False, False)
            with pe.Fori(1, T // 2 - 1) as q:
                for par in range(2):
                    row_block(2 * q + par, par, False, False, True)
            row_block(T - 2, 0, False, False, True)
            row_block(T - 1, 1, False, True, True)

            def group(g, par, first):
                if first and par == 0:
                    pe.wait_ge(fin, FIN * T - FIN - FIN + 4)
                    pe.wait_ge(y_step, YST * (T - 1))
                if first and par == 1:
                    pe.wait_ge(fin, FIN * T)
                if not first:
                    pe.wait_ge(spec_step, SPEC * g - 2 * SPEC + 1)
                for k in range(NPC):
                    pe.wait_ge(piece_loaded[k % RING], 32 * g + 16 * (k // RING) + 16)
                    if first and par == 0 and k == NPC - 1:
                        pe.wait_ge(y_step, YST * T)
                    passed(pe, "pe")
                    for r in range(PI):
                        it = k * PI + r
                        for jt in range(BT):
                            last = pe.matmul(bank[4 * par + jt // 2][:, (jt % 2) * 2 * C:(jt % 2 + 1) * 2 * C],
                                             piece[:, k % RING, r, jt * P:(jt + 1) * P], y[:, it, :],
                                             start=(it == 0 and jt % 2 == 0), stop=(it == T - 1),
                                             skip_group_check=True)
                    last.then_inc(piece_used, 1)

            group(0, 0, True)
            group(1, 1, True)
            with pe.Fori(1, G // 2) as q:
                for par in range(2):
                    group(2 * q + par, par, False)

            def rows(ib, k, first):
                pe.wait_ge(slab_loaded[k], (4 * (ib - k)) + 16)
                if not first:
                    pe.wait_ge(fin3, FIN3 * ib - RING * FIN3 + 1)
                passed(pe, "pe")
                for t in range(T):
                    last = pe.matmul(bank[k][:, 0:2 * C], slab[:, k, t * P:(t + 1) * P], z2[:, t, :],
                                     start=(t == 0), stop=(t == T - 1))
                last.then_inc(rows_done, 1)

            pe.wait_ge(z2_ready, G)
            for k in range(RING):
                rows(k, k, True)
            with pe.Fori(1, T // RING) as q:
                for k in range(RING):
                    rows(RING * q + k, k, False)


def kernel(**inputs):
    import numpy as np
    import concourse.bacc as bacc
    from concourse import mybir as mb
    from concourse.bass_utils import run_bass_kernel_spmd as run

    nc = bacc.Bacc("TRN2", target_bir_lowering=False, num_devices=1)
    a = {k: np.asarray(v) for k, v in inputs.items()}
    n = a["x"].shape[0]
    laid_out = {
        "adj": a["adj"],
        "x": a["x"],
        "in2T": a["L0_gnn_inlayer2"].T,
        "W1": a["L0_gnn_W1"],
        "w23": np.stack([a["L0_gnn_w2"], a["L0_gnn_w3"]], axis=1),
        "b23": np.stack([a["L0_gnn_b2"], a["L0_gnn_b3"]]).reshape(2),
        "mass_t": a["L1_gnn_mass"].reshape(n // P, P).T,
        "evals0": a["L1_gnn_evals0"],
        "evals1": a["L1_gnn_evals1"].reshape(P, 1),
        "dt_rows": a["L1_gnn_diffusion_time"],
    }
    arrays, args = {}, []
    for name, v in laid_out.items():
        v = np.ascontiguousarray(v)
        arrays[f"in_{name}"] = v
        args.append(nc.dram_tensor(f"in_{name}", v.shape, mb.dt.from_np(v.dtype), kind="ExternalInput").ap())
    out = nc.dram_tensor("out_0", a["x"].shape, mb.dt.float32, kind="ExternalOutput").ap()
    build(nc, *args, out)
    r = run(nc, [arrays], core_ids=[0])
    return r.results[0]["out_0"]
```

```python
import concourse.bass as bass
from concourse import mybir
from contextlib import ExitStack

P = 128


def build(nc, adj, x, in2T, W1, w23, b23, mass_t, evals0, evals1, dt_rows, out):
    fp32, bf16, fp16 = mybir.dt.float32, mybir.dt.bfloat16, mybir.dt.float16
    fp8, u8, u16 = mybir.dt.float8e4, mybir.dt.uint8, mybir.dt.uint16
    ALU, ACT, AX = mybir.AluOpType, mybir.ActivationFunctionType, mybir.AxisListType

    N, C = x.shape
    EMB2 = in2T.shape[0]
    KE = EMB2 // P
    T = N // P
    BT = 8
    BW = BT * P
    NB = T // BT
    NC = NB // 2
    LEAD = 3
    LB = 4
    HB = NB // 2
    Z = 2 * (C + 1)
    ZL = C + 1
    LO = 2.0 ** 11
    ZS = 2.0 ** 6
    YS = 2.0 ** 8
    GS = 2.0 ** -2
    EPS = 1e-5
    SLOPE = 0.01
    EDGE = 0x3F80
    EDGE8 = 1.875
    G = NB
    PI = 8
    NPC = T // PI
    RING = 4

    adjT8 = nc.dram_tensor("adjT8", (T, P, T * P), u8, kind="Internal").ap()
    adj8 = nc.dram_tensor("adj8", (T, P, T * P), u8, kind="Internal").ap()
    adj8_g = adj8.rearrange("t p (g j) -> g t p j", g=G)
    x1_d = nc.dram_tensor("x1_d", (T, P, C), fp32, kind="Internal").ap()
    f2_d = nc.dram_tensor("f2_d", (T, P), fp32, kind="Internal").ap()
    x_t = x.rearrange("(t p) c -> t p c", p=P)
    out_t = out.rearrange("(t p) c -> t p c", p=P)
    adj_t = adj.rearrange("(t p) j -> t p j", p=P)

    ctx = ExitStack()
    with ctx:
        def sb(name, shape, dt):
            return ctx.enter_context(nc.sbuf_tensor(name, shape, dt))

        def sem(name):
            return ctx.enter_context(nc.semaphore(name))

        f2_region = sb("f2_region", [P, N * 4], u8)
        f2row = f2_region[:, :].bitcast(fp32)
        piece_b = f2_region[:, :].rearrange("p (r t j) -> p r t j", r=RING, t=PI)
        piece = f2_region[:, :].bitcast(fp8).rearrange("p (r t j) -> p r t j", r=RING, t=PI)
        z_region = sb("z_region", [P, T * 2 * Z * 2], u8)
        z = z_region[:, :].bitcast(fp16).rearrange("p (t m c) -> p t m c", m=2, c=Z)
        in2 = z_region[:, 0:KE * N * 4].bitcast(fp32).rearrange("p (k n) -> p k n", k=KE)
        z2 = z_region[:, 0:T * 2 * C * 2].bitcast(fp16).rearrange("p (t c) -> p t c", t=T)
        slab_b = z_region[:, N * 4:N * 4 + RING * N].rearrange("p (r j) -> p r j", r=RING)
        slab = z_region[:, N * 4:N * 4 + RING * N].bitcast(fp8).rearrange("p (r j) -> p r j", r=RING)
        y_region = sb("y_region", [P, T * 2 * C * 2], u8)
        y = y_region[:, :].bitcast(fp16).rearrange("p (t c) -> p t c", t=T)
        x_all = y_region[:, :].bitcast(fp32).rearrange("p (t c) -> p t c", t=T)
        stage = sb("stage", [P, NB, BW], fp32)
        adj_hi = stage[:, :, :].bitcast(u16).rearrange("p b (j h) -> p b j h", h=2)[:, :, :, 1]
        wide_f = [stage[:, k, :].rearrange("p (t c) -> p t c", t=BT) for k in range(3)]
        adj_b = stage[:, :, :].rearrange("p b j -> p (b j)").bitcast(u8).rearrange(
            "p (c j h) -> p c j h", c=NC, h=4)[:, :, :, 3]
        zt_region = sb("zt_region", [P, 2 * BT * C * 4], u8)
        zt = zt_region[:, :].bitcast(fp32).rearrange("p (m t c) -> p m t c", m=2, t=BT)
        packed = zt_region[:, 0:N].rearrange("p (h j) -> p h j", h=2)
        label = sb("label", [P, LB, BW], u16)
        label_t = label[:, :, :].bitcast(bf16)
        labT = sb("labT", [P, 2, BW], u16)
        m_pos = sb("m_pos", [P, 2, BW], bf16)
        m_neg = sb("m_neg", [P, 2, BW], bf16)
        aT_half = sb("aT_half", [P, 2, HB * BW], u8)
        ident = sb("ident", [P, P], bf16)
        prep = m_neg[:, :, :].rearrange("p a b -> p (a b)").bitcast(fp32)
        identf, inv_n, ones, f2T, w1s = (prep[:, 0:P], prep[:, P:2 * P], prep[0:1, 2 * P:3 * P],
                                         prep[0:T, 3 * P:4 * P], prep[:, 4 * P:4 * P + EMB2])
        w23s = sb("w23s", [P, 2], fp32)
        b23s = sb("b23s", [P, 2], fp32)
        v23 = sb("v23", [P, KE, 2], fp32)
        f1 = sb("f1", [P, T], fp32)
        nf1 = sb("nf1", [P, T], fp32)
        f2 = sb("f2", [P, T], fp32)
        top = sb("top", [P, 1], fp32)
        top1 = sb("top1", [1, 1], fp32)
        F2 = sb("F2", [P, 1], fp32)
        tmp_a = sb("tmp_a", [P, T], fp32)
        tmp_b = sb("tmp_b", [P, T], fp32)
        row_pos = sb("row_pos", [P, 2, T], fp32)
        row_neg = sb("row_neg", [P, 2, T], fp32)
        f2s = sb("f2s", [P, T], fp32)
        wj = sb("wj", [P, 2, T], fp32)
        mass = sb("mass", [P, T], fp32)
        xmean = sb("xmean", [P, C], fp32)
        eps = sb("eps", [P, 1], fp32)
        ev0 = sb("ev0", [P, T], fp32)
        ev1 = sb("ev1", [P, 1], fp32)
        dts = sb("dts", [P, 2, C], fp32)
        e1 = sb("e1", [P, C], fp32)
        xt = sb("xt", [P, 2, C], fp32)
        u = sb("u", [P, ZL], fp32)
        col = sb("col", [P, 4], fp32)
        tt = sb("tt", [P, C], fp32)
        st = sb("st", [P, 6], fp32)
        mv = sb("mv", [P, 2], fp32)
        sd = sb("sd", [P, 1], fp32)
        x1 = sb("x1", [P, 2, C], fp32)
        ym = sb("ym", [P, C], fp32)

        bank = [ctx.enter_context(nc.psum_tensor(f"bank{k}", [P, 512], fp32)) for k in range(8)]
        tp = [bank[4 + k][:, :].bitcast(bf16) for k in range(4)]
        tp_u16 = [bank[4 + k][:, :].bitcast(u16) for k in range(4)]
        tp_hi8 = [bank[4 + k][:, :].bitcast(fp8).rearrange("p (j h) -> p j h", h=2)[:, :, 1] for k in range(4)]

        def acc(ib_par, m):
            return bank[2 * ib_par + m][:, 0:Z]

        weights_loaded, consts_loaded, x_loaded = map(sem, ("weights_loaded", "consts_loaded", "x_loaded"))
        in2_loaded = [sem(f"in2_loaded{k}") for k in range(NB)]
        ident_step, ones_ready = sem("ident_step"), sem("ones_ready")
        v_summed, v_ready, fcol_summed, top_turned, top_spread, f2T_turned, f2T_ready, f2_stored, frow_loaded = map(
            sem, ("v_summed", "v_ready", "fcol_summed", "top_turned", "top_spread", "f2T_turned", "f2T_ready",
                  "f2_stored", "frow_loaded"))
        mean_summed, mean_ready, dve_prep, act_prep = map(sem, ("mean_summed", "mean_ready", "dve_prep", "act_prep"))
        zt_ready = [sem(f"zt_ready{m}") for m in range(2)]
        zhi_ready, zd_ready, zlo_ready = map(sem, ("zhi_ready", "zd_ready", "zlo_ready"))
        adj_loaded = [sem(f"adj_loaded{k}") for k in range(NC)]
        pack_ready = sem("pack_ready")
        pack_stored = [sem(f"pack_stored{k}") for k in range(2)]
        label_ready, transposed, labT_ready, aT_ready, masks_ready, multiplied = map(sem, (
            "label_ready", "transposed", "labT_ready", "aT_ready", "masks_ready", "multiplied"))
        aT_stored = [sem(f"aT_stored{k}") for k in range(2)]
        xt_loaded = [sem(f"xt_loaded{k}") for k in range(2)]
        x1_stored = [sem(f"x1_stored{k}") for k in range(2)]
        fin, sd_ready, y_step = sem("fin"), sem("sd_ready"), sem("y_step")
        piece_loaded = [sem(f"piece_loaded{k}") for k in range(RING)]
        piece_used = sem("piece_used")
        lo_ready, spec_step, e_arg_ready, e_ready, zh2_ready, z2_ready = map(sem, (
            "lo_ready", "spec_step", "e_arg_ready", "e_ready", "zh2_ready", "z2_ready"))
        slab_loaded = [sem(f"slab_loaded{k}") for k in range(RING)]
        rows_done, lo3_ready, fin3, sd3_ready = map(sem, ("rows_done", "lo3_ready", "fin3", "sd3_ready"))
        xr_loaded = [sem(f"xr_loaded{k}") for k in range(2)]
        out_stored = [sem(f"out_stored{k}") for k in range(2)]

        FIN = 13
        FIN3 = 6
        SPEC = 4
        YST = 3

        block = ctx.enter_context(nc.Block())

        def ab(t, shape):
            return t.to_broadcast(shape)

        waits_passed = {n: sem(f"waits_passed_{n}") for n in ("sp", "pool", "dve", "pe")}

        def passed(eng, name):
            eng.sem_inc(waits_passed[name], 1)

        @block.sync
        def _(sp):
            sp.dma_start(w1s[:, :], W1).then_inc(weights_loaded, 16)
            sp.dma_start(w23s[:, :], w23).then_inc(weights_loaded, 16)
            sp.dma_start(b23s[:, :], b23.partition_broadcast(P)).then_inc(weights_loaded, 16)
            for s in range(NB):
                sp.dma_start(in2[:, :, s * BW:(s + 1) * BW],
                             in2T[:, s * BW:(s + 1) * BW].rearrange("(k p) n -> p k n", p=P)
                             ).then_inc(in2_loaded[s], 16)
            sp.dma_start(x_all, x.rearrange("(t p) c -> p t c", p=P)).then_inc(x_loaded, 16)

            def load_adj(ib, c):
                sp.dma_start(stage[:, 2 * c:2 * c + 2, :],
                             adj_t[ib, :, 2 * c * BW:(2 * c + 2) * BW].rearrange("p (b j) -> p b j", b=2)
                             ).then_inc(adj_loaded[c], 16)

            for c in range(NC):
                load_adj(0, c)
            sp.wait_ge(f2T_ready, 1)
            sp.dma_start(f2_d, f2T[:, :]).then_inc(f2_stored, 16)
            sp.wait_ge(f2_stored, 16)
            sp.dma_start(f2row, f2_d.rearrange("t p -> (t p)").partition_broadcast(P)).then_inc(frow_loaded, 16)

            def row_block(ib, last):
                for c in range(NC):
                    sp.wait_ge(label_ready, NB * ib + 2 * c + 2)
                    passed(sp, "sp")
                    sp.wait_ge(pack_ready, NC * ib + c + 1)
                    passed(sp, "sp")
                    if not last:
                        load_adj(ib + 1, c)
                    if c % 2 == 1:
                        sp.dma_start(adj8[ib, :, c // 2 * HB * BW:(c // 2 + 1) * HB * BW], packed[:, c // 2, :]
                                     ).then_inc(pack_stored[c // 2], 16)

            row_block(0, False)
            with sp.Fori(1, T - 1) as ib:
                row_block(ib, False)
            row_block(T - 1, True)

            sp.wait_ge(label_ready, NB * T)

            def load_piece(g, k, reuse):
                if reuse:
                    sp.wait_ge(piece_used, NPC * g + k - RING + 1)
                passed(sp, "sp")
                sp.dma_start(piece_b[:, k % RING],
                             adj8_g[g, k * PI:(k + 1) * PI].rearrange("t p j -> p t j")
                             ).then_inc(piece_loaded[k % RING], 16)

            for k in range(NPC):
                if k == NPC - 1:
                    for h in range(2):
                        sp.wait_ge(pack_stored[h], 16 * T)
                elif k == 0:
                    sp.wait_ge(pack_stored[0], 16 * (T - 1))
                load_piece(0, k, k >= RING)
            with sp.Fori(1, G) as g:
                for k in range(NPC):
                    load_piece(g, k, True)

            for h in range(2):
                sp.wait_ge(aT_stored[h], 16 * T)
                sp.wait_ge(x1_stored[h], 16 * (T // 2))
            sp.wait_ge(multiplied, NB * T)

            def out_store(ib, par):
                sp.wait_ge(fin3, FIN3 * ib + FIN3)
                passed(sp, "sp")
                sp.dma_start(out_t[ib], x1[:, par, :]).then_inc(out_stored[par], 16)

            def load_slab(ib, k, first):
                if not first:
                    sp.wait_ge(rows_done, ib - RING + 1)
                passed(sp, "sp")
                sp.dma_start(slab_b[:, k, :], adjT8[ib]).then_inc(slab_loaded[k], 16)

            def load_x1(ib, par, first):
                if not first:
                    sp.wait_ge(fin3, FIN3 * (ib - 2) + 2)
                passed(sp, "sp")
                sp.dma_start(xt[:, par, :], x1_d[ib]).then_inc(xr_loaded[par], 16)

            sp.wait_ge(fin, FIN * T)
            for k in range(RING):
                load_slab(k, k, True)
            for k in range(2):
                load_x1(k, k, True)
            with sp.Fori(0, T // RING - 1) as q:
                for k in range(RING):
                    ib = RING * q + k
                    out_store(ib, k % 2)
                    load_x1(ib + 2, k % 2, False)
                    load_slab(ib + RING, k, False)
            for k in range(RING):
                ib = T - RING + k
                out_store(ib, k % 2)
                if k < 2:
                    load_x1(ib + 2, k % 2, False)
            for par in range(2):
                sp.wait_ge(out_stored[par], 16 * (T // 2))

        @block.gpsimd
        def _(pool):
            pool.memset(ident[:, :], 0.0).then_inc(ident_step, 1)
            pool.memset(identf[:, :], 0.0).then_inc(ident_step, 1)
            pool.memset(inv_n[:, :], 1.0 / N).then_inc(ones_ready, 1)
            pool.memset(ones[:, :], 1.0).then_inc(ones_ready, 1)
            pool.memset(eps[:, :], EPS).then_inc(ones_ready, 1)
            pool.wait_ge(ident_step, 2)
            for m in (ident, identf):
                pool.affine_select(out=m[:, :], in_=m[:, :], compare_op=ALU.not_equal, fill=1.0,
                                   base=0, pattern=[[-1, P]], channel_multiplier=1).then_inc(ident_step, 1)
            pool.dma_start(mass[:, :], mass_t).then_inc(consts_loaded, 16)
            pool.dma_start(ev0[:, :], evals0.partition_broadcast(P)).then_inc(consts_loaded, 16)
            pool.dma_start(ev1[:, :], evals1).then_inc(consts_loaded, 16)
            pool.dma_start(dts[:, :, :], dt_rows.partition_broadcast(P)).then_inc(consts_loaded, 16)

            pool.wait_ge(x_loaded, 16)
            pool.wait_ge(dve_prep, 12)
            for h in range(NB):
                if h >= 1:
                    pool.wait_ge(zlo_ready, 2 * h)
                pool.tensor_tensor(zt[:, 1], x_all[:, h * BT:(h + 1) * BT, :],
                                   wj[:, 1, h * BT:(h + 1) * BT].unsqueeze(2).to_broadcast([P, BT, C]),
                                   ALU.mult).then_inc(zt_ready[1], 1)

            def load_xt(ib, par, first):
                if not first:
                    pool.wait_ge(fin, FIN * (ib - 2) + 9)
                pool.dma_start(xt[:, par, :], x_t[ib]).then_inc(xt_loaded[par], 16)

            def store_x1(ib, par):
                pool.wait_ge(fin, FIN * ib + FIN)
                passed(pool, "pool")
                pool.dma_start(x1_d[ib], x1[:, par, :]).then_inc(x1_stored[par], 16)

            def y_of(ib, par, first=False):
                if not first:
                    pool.wait_ge(y_step, YST * ib)
                pool.wait_ge(fin, FIN * ib + FIN)
                pool.tensor_tensor(ym[:, :], x1[:, par, :], ab(mass[:, bass.ds(ib, 1)], [P, C]), ALU.mult
                                   ).then_inc(y_step, 1)
                pool.wait_ge(y_step, YST * ib + 1)
                pool.tensor_copy(y[:, ib, 0:C], ym[:, :]
                                 ).then_inc(y_step, 1)
                pool.wait_ge(y_step, YST * ib + 2)
                pool.tensor_tensor(y[:, ib, C:2 * C], ym[:, :], y[:, ib, 0:C], ALU.subtract
                                   ).then_inc(y_step, 1)

            pool.wait_ge(zlo_ready, 2 * NB)
            pool.wait_ge(mean_ready, 1)
            def pack(ib, c, first):
                pool.wait_ge(adj_loaded[c], 16 * ib + 16)
                if c % 2 == 0 and not first:
                    pool.wait_ge(pack_stored[c // 2], 16 * ib)
                passed(pool, "pool")
                pool.affine_select(out=packed[:, c // 2, c % 2 * 2 * BW:(c % 2 + 1) * 2 * BW], in_=adj_b[:, c, :],
                                   compare_op=ALU.not_equal, fill=0, base=1, pattern=[[0, 2 * BW]],
                                   channel_multiplier=0).then_inc(pack_ready, 1)

            def row_block(ib, par, first=False):
                pack(ib, 0, False)
                pack(ib, 1, False)
                load_xt(ib, par, first)
                pack(ib, 2, False)
                pack(ib, 3, False)
                store_x1(ib - 1, 1 - par)
                y_of(ib - 1, 1 - par, first)

            for c in range(NC):
                pack(0, c, True)
            load_xt(0, 0, True)
            row_block(1, 1, True)
            with pool.Fori(1, T // 2) as q:
                for par in range(2):
                    row_block(2 * q + par, par)
            store_x1(T - 1, 1)
            y_of(T - 1, 1)

        @block.scalar
        def _(act):
            act.wait_ge(f2T_turned, 1)
            act.activation(f2T[:, :], bank[5][0:T, 0:P], ACT.Copy).then_inc(f2T_ready, 1)
            act.wait_ge(dve_prep, 8)
            act.activation(row_pos[:, 0, :], tmp_a[:, :], ACT.Exp, scale=1.0 - SLOPE).then_inc(act_prep, 1)
            act.activation(row_neg[:, 0, :], tmp_b[:, :], ACT.Exp, scale=SLOPE - 1.0).then_inc(act_prep, 1)
            act.activation(wj[:, 0, :], f2s[:, :], ACT.Exp).then_inc(act_prep, 1)
            act.activation(wj[:, 1, :], f2s[:, :], ACT.Exp, scale=SLOPE).then_inc(act_prep, 1)
            act.wait_ge(dve_prep, 10)
            act.activation(e1[:, :], e1[:, :], ACT.Exp, scale=-1.0).then_inc(act_prep, 1)
            def split_high(h, m):
                act.wait_ge(zt_ready[m], h + 1)
                act.activation(z[:, h * BT:(h + 1) * BT, m, 0:C], zt[:, m], ACT.Copy).then_inc(zhi_ready, 1)

            def split_low(h, m):
                act.wait_ge(zd_ready, 2 * h + m + 1)
                act.activation(z[:, h * BT:(h + 1) * BT, m, ZL:ZL + C], zt[:, m], ACT.Copy, scale=LO
                               ).then_inc(zlo_ready, 1)

            def split(h):
                for m in range(2):
                    split_high(h, m)
                for m in range(2):
                    split_low(h, m)

            def bank_out(ib, b, first):
                n = NB * ib + b
                act.wait_ge(transposed, n + 1)
                if not (first and b < 2):
                    act.wait_ge(masks_ready, n - 1)
                if not first and b % HB == 0:
                    act.wait_ge(aT_stored[b // HB], 16 * ib)
                act.activation(labT[:, b % 2, :], tp_u16[b % 4], ACT.Copy).then_inc(labT_ready, 1)
                dst = aT_half[:, b // HB, (b % HB) * BW:(b % HB + 1) * BW].bitcast(fp8)
                act.activation(dst, tp_hi8[b % 4], ACT.Copy, scale=1.0 / EDGE8, saturate=False
                               ).then_inc(aT_ready, 1)

            def store_aT(ib, h):
                act.wait_ge(aT_ready, NB * ib + HB * (h + 1))
                act.dma_start(adjT8[ib, :, h * HB * BW:(h + 1) * HB * BW], aT_half[:, h, :]
                              ).then_inc(aT_stored[h], 16)

            def deviation(ib):
                act.wait_ge(fin, FIN * ib + 11)
                act.activation(sd[:, :], mv[:, 1:2], ACT.Sqrt, bias=eps[:, :]).then_inc(sd_ready, 1)

            def row_block(ib, first):
                for b in range(NB):
                    bank_out(ib, b, first)
                    if b == 0 and not first:
                        store_aT(ib - 1, 1)
                    if b == HB:
                        store_aT(ib, 0)
                    if b == NB - 1 and not first:
                        deviation(ib - 1)

            for h in range(NB):
                split(h)
                if h >= 4:
                    bank_out(0, h - 4, True)
            for b in range(NB - 4, NB):
                bank_out(0, b, True)
                if b == HB:
                    store_aT(0, 0)
            act.wait_ge(ones_ready, 3)
            with act.Fori(1, T) as ib:
                row_block(ib, False)
            store_aT(T - 1, 1)
            deviation(T - 1)

            def group(g, par, first):
                act.wait_ge(piece_used, NPC * g + NPC)
                if not first:
                    act.wait_ge(spec_step, SPEC * g)
                for k in range(4):
                    act.activation(wide_f[0][:, 2 * k:2 * k + 2, :],
                                   bank[4 - 4 * par + k][:, :].rearrange("p (t c) -> p t c", t=2)[:, :, C:2 * C],
                                   ACT.Copy, scale=1.0 / (YS * EDGE8)).then_inc(lo_ready, 1)
                act.wait_ge(e_arg_ready, g + 1)
                act.activation(wide_f[1], wide_f[1], ACT.Exp, scale=-1.0).then_inc(e_ready, 1)
                act.wait_ge(spec_step, SPEC * g + 3)
                act.activation(z2[:, bass.ds(g * BT, BT), 0:C], wide_f[0], ACT.Copy, scale=GS
                               ).then_inc(zh2_ready, 1)
                act.wait_ge(spec_step, SPEC * g + 4)
                act.activation(z2[:, bass.ds(g * BT, BT), C:2 * C], wide_f[2], ACT.Copy, scale=LO
                               ).then_inc(z2_ready, 1)

            for par in range(2):
                group(par, par, par == 0)
            with act.Fori(1, G // 2) as q:
                for par in range(2):
                    group(2 * q + par, par, False)

            def finish(ib, k):
                act.wait_ge(rows_done, ib + 1)
                act.activation(u[:, 0:C], bank[4 + k][:, C:2 * C], ACT.Copy, scale=1.0 / (LO * GS)
                               ).then_inc(lo3_ready, 1)
                act.wait_ge(fin3, FIN3 * ib + 4)
                act.activation(sd[:, :], mv[:, 1:2], ACT.Sqrt, bias=eps[:, :]).then_inc(sd3_ready, 1)

            for k in range(RING):
                finish(k, k)
            with act.Fori(1, T // RING) as q:
                for k in range(RING):
                    finish(RING * q + k, k)

        @block.vector
        def _(dve):
            dve.wait_ge(v_summed, 1)
            dve.tensor_copy(v23[:, :, :], bank[1][:, 0:2 * KE].rearrange("p (k w) -> p k w", k=KE)
                            ).then_inc(v_ready, 1)
            dve.wait_ge(weights_loaded, 48)
            dve.wait_ge(fcol_summed, 1)
            fc = bank[0][:, 0:2 * T].rearrange("p (t w) -> p t w", w=2)
            dve.tensor_scalar(f2[:, :], fc[:, :, 1], b23s[:, 1:2], None, ALU.add).then_inc(dve_prep, 1)
            dve.wait_ge(dve_prep, 1)
            dve.reduce_max(top[:, :], f2[:, :], axis=AX.X).then_inc(dve_prep, 1)
            dve.tensor_scalar(f1[:, :], fc[:, :, 0], b23s[:, 0:1], None, ALU.add).then_inc(dve_prep, 1)
            dve.wait_ge(top_turned, 1)
            dve.reduce_max(top1[:, :], bank[6][0:1, 0:P], axis=AX.X).then_inc(dve_prep, 1)
            dve.wait_ge(top_spread, 1)
            dve.tensor_copy(F2[:, :], bank[7][:, 0:1]).then_inc(dve_prep, 1)
            dve.wait_ge(dve_prep, 5)
            dve.tensor_scalar(tmp_a[:, :], f1[:, :], F2[:, :], 0.0, ALU.add, ALU.min).then_inc(dve_prep, 1)
            dve.tensor_scalar(tmp_b[:, :], f1[:, :], F2[:, :], 0.0, ALU.add, ALU.max).then_inc(dve_prep, 1)
            dve.tensor_scalar(f2s[:, :], f2[:, :], F2[:, :], None, ALU.subtract).then_inc(dve_prep, 1)
            dve.tensor_scalar(nf1[:, :], f1[:, :], -1.0, None, ALU.mult).then_inc(dve_prep, 1)
            dve.wait_ge(consts_loaded, 64)
            dve.tensor_scalar(e1[:, :], dts[:, 1, :], ev1[:, :], None, ALU.mult).then_inc(dve_prep, 1)
            dve.tensor_scalar(mass[:, :], mass[:, :], YS, None, ALU.mult).then_inc(dve_prep, 1)
            dve.wait_ge(act_prep, 4)
            dve.tensor_scalar(wj[:, :, :], wj[:, :, :], ZS, None, ALU.mult).then_inc(dve_prep, 1)
            for r in (row_pos, row_neg):
                dve.tensor_scalar(r[:, 1, :], r[:, 0, :], 1.0 / (ZS * LO), None, ALU.mult).then_inc(dve_prep, 1)
            dve.wait_ge(dve_prep, 14)
            for r in (row_pos, row_neg):
                dve.tensor_scalar(r[:, 0, :], r[:, 0, :], 1.0 / ZS, None, ALU.mult).then_inc(dve_prep, 1)
            for m in range(2):
                dve.tensor_copy(z[:, :, m, C], wj[:, m, :]).then_inc(dve_prep, 1)
            dve.wait_ge(dve_prep, 18)
            for m, d in enumerate((tmp_a, tmp_b)):
                dve.tensor_tensor(d[:, :], wj[:, m, :], z[:, :, m, C], ALU.subtract).then_inc(dve_prep, 1)
            dve.wait_ge(dve_prep, 20)
            for m, d in enumerate((tmp_a, tmp_b)):
                dve.tensor_scalar(z[:, :, m, C + ZL], d[:, :], LO, None, ALU.mult).then_inc(dve_prep, 1)
            dve.wait_ge(x_loaded, 16)

            def table_product(h):
                if h >= 1:
                    dve.wait_ge(zlo_ready, 2 * h - 1)
                dve.tensor_tensor(zt[:, 0], x_all[:, h * BT:(h + 1) * BT, :],
                                  wj[:, 0, h * BT:(h + 1) * BT].unsqueeze(2).to_broadcast([P, BT, C]),
                                  ALU.mult).then_inc(zt_ready[0], 1)

            def table_rest(h, m):
                dve.wait_ge(zhi_ready, 2 * h + m + 1)
                dve.tensor_tensor(zt[:, m], zt[:, m], z[:, h * BT:(h + 1) * BT, m, 0:C], ALU.subtract
                                  ).then_inc(zd_ready, 1)

            def make_label(ib, b, fresh):
                if b % 2 == 0:
                    dve.wait_ge(adj_loaded[b // 2], 16 * ib + 16)
                dve.scalar_tensor_tensor(label[:, b % LB, :], f2row[:, b * BW:(b + 1) * BW], nf1[:, bass.ds(ib, 1)],
                                         adj_hi[:, b, :], ALU.is_gt, ALU.add).then_inc(label_ready, 1)

            def masks(ib, b, fresh):
                n = NB * ib + b
                dve.wait_ge(labT_ready, n + 1)
                if not (fresh and b < 2):
                    dve.wait_ge(multiplied, n - 1)
                dve.tensor_scalar(m_pos[:, b % 2, :], labT[:, b % 2, :], float(EDGE + 1), None, ALU.is_equal)
                dve.tensor_scalar(m_neg[:, b % 2, :], labT[:, b % 2, :], float(EDGE), None, ALU.is_equal
                                  ).then_inc(masks_ready, 1)

            def finish(ib, par, step, reuse):
                n = FIN * ib
                pos, neg = acc(par, 0), acc(par, 1)
                one = bass.ds(ib, 1)
                if step == 0:
                    dve.wait_ge(multiplied, NB * ib + NB)
                    dve.tensor_scalar(u[:, :], pos[:, 0:ZL], row_pos[:, 0, one], None, ALU.mult).then_inc(fin, 1)
                elif step == 1:
                    dve.wait_ge(fin, n + 1)
                    dve.scalar_tensor_tensor(u[:, :], pos[:, ZL:Z], row_pos[:, 1, one], u[:, :], ALU.mult, ALU.add
                                             ).then_inc(fin, 1)
                elif step == 2:
                    dve.wait_ge(fin, n + 2)
                    dve.scalar_tensor_tensor(u[:, :], neg[:, 0:ZL], row_neg[:, 0, one], u[:, :], ALU.mult, ALU.add
                                             ).then_inc(fin, 1)
                elif step == 3:
                    dve.wait_ge(fin, n + 3)
                    dve.scalar_tensor_tensor(u[:, :], neg[:, ZL:Z], row_neg[:, 1, one], u[:, :], ALU.mult, ALU.add
                                             ).then_inc(fin, 1)
                elif step == 4:
                    dve.wait_ge(fin, n + 4)
                    dve.tensor_scalar(col[:, 0:1], u[:, C:ZL], 0.0, None, ALU.is_le).then_inc(fin, 1)
                elif step == 5:
                    dve.wait_ge(fin, n + 5)
                    dve.tensor_tensor(col[:, 1:2], u[:, C:ZL], col[:, 0:1], ALU.add).then_inc(fin, 1)
                elif step == 6:
                    dve.wait_ge(fin, n + 6)
                    dve.reciprocal(col[:, 2:3], col[:, 1:2]).then_inc(fin, 1)
                elif step == 7:
                    dve.scalar_tensor_tensor(tt[:, :], xmean[:, :], col[:, 0:1], u[:, 0:C], ALU.mult, ALU.add
                                             ).then_inc(fin, 1)
                elif step == 8:
                    dve.wait_ge(fin, n + 8)
                    dve.wait_ge(xt_loaded[par], 8 * (ib - par) + 16)
                    dve.scalar_tensor_tensor(tt[:, :], tt[:, :], col[:, 2:3], xt[:, par, :], ALU.mult, ALU.add
                                             ).then_inc(fin, 1)
                elif step == 9:
                    dve.wait_ge(fin, n + 9)
                    dve.bn_stats(st[:, :], tt[:, :]).then_inc(fin, 1)
                elif step == 10:
                    dve.wait_ge(fin, n + 10)
                    passed(dve, "dve")
                    dve.bn_aggr(mv[:, :], st[:, :]).then_inc(fin, 1)
                elif step == 11:
                    dve.wait_ge(sd_ready, ib + 1)
                    dve.reciprocal(col[:, 3:4], sd[:, :]).then_inc(fin, 1)
                else:
                    dve.wait_ge(fin, n + 12)
                    if reuse:
                        dve.wait_ge(x1_stored[par], 8 * (ib - par))
                        dve.wait_ge(y_step, YST * ib - 2 * YST + 1)
                    dve.tensor_scalar(x1[:, par, :], tt[:, :], mv[:, 0:1], col[:, 3:4], ALU.subtract, ALU.mult
                                      ).then_inc(fin, 1)

            AFTER_MASKS = ((), (0,), (2,), (4,), (6, 7), (9,), (), ())
            AFTER_LABEL = ((), (1,), (3,), (5,), (8,), (10,), (), (11, 12))

            def row_block(ib, par, last, reuse):
                for b in range(NB):
                    masks(ib, b, False)
                    for step in AFTER_MASKS[b]:
                        finish(ib - 1, 1 - par, step, reuse)
                    if b + LEAD < NB:
                        make_label(ib, b + LEAD, False)
                    elif not last:
                        make_label(ib + 1, b + LEAD - NB, False)
                    for step in AFTER_LABEL[b]:
                        finish(ib - 1, 1 - par, step, reuse)

            table_product(0)
            for h in range(NB):
                table_rest(h, 0)
                table_rest(h, 1)
                if h + 1 < NB:
                    table_product(h + 1)
                if h == 3:
                    dve.wait_ge(frow_loaded, 16)
                if h >= 3:
                    make_label(0, h - 3, True)
                if h >= 5:
                    masks(0, h - 5, True)
            dve.wait_ge(mean_summed, 1)
            dve.tensor_copy(xmean[:, :], bank[2][:, 0:C]).then_inc(mean_ready, 1)
            make_label(0, 5, True)
            for b in range(3, NB):
                masks(0, b, True)
                if b + LEAD < NB:
                    make_label(0, b + LEAD, True)
                else:
                    make_label(1, b + LEAD - NB, False)
            row_block(1, 1, False, False)
            row_block(2, 0, False, False)
            row_block(3, 1, False, True)
            with dve.Fori(2, T // 2 - 1) as q:
                for par in range(2):
                    row_block(2 * q + par, par, False, True)
            row_block(T - 2, 0, False, True)
            row_block(T - 1, 1, True, True)
            for step in range(FIN):
                finish(T - 1, 1, step, True)

            def spectrum(g, par, first):
                n = SPEC * g
                if not first:
                    dve.wait_ge(z2_ready, g)
                dve.tensor_tensor(wide_f[1], dts[:, 0, :].unsqueeze(1).to_broadcast([P, BT, C]),
                                  ev0[:, bass.ds(g * BT, BT)].unsqueeze(2).to_broadcast([P, BT, C]), ALU.mult
                                  ).then_inc(e_arg_ready, 1)
                for k in range(4):
                    dve.wait_ge(lo_ready, 4 * g + k + 1)
                    last = dve.scalar_tensor_tensor(
                        wide_f[0][:, 2 * k:2 * k + 2, :],
                        bank[4 - 4 * par + k][:, :].rearrange("p (t c) -> p t c", t=2)[:, :, 0:C],
                        1.0 / (YS * EDGE8),
                        wide_f[0][:, 2 * k:2 * k + 2, :], ALU.mult, ALU.add)
                last.then_inc(spec_step, 1)
                dve.wait_ge(spec_step, n + 1)
                dve.tensor_tensor(wide_f[0], wide_f[0], e1[:, :].unsqueeze(1).to_broadcast([P, BT, C]), ALU.mult
                                  ).then_inc(spec_step, 1)
                dve.wait_ge(spec_step, n + 2)
                dve.wait_ge(e_ready, g + 1)
                dve.tensor_tensor(wide_f[0], wide_f[0], wide_f[1], ALU.mult).then_inc(spec_step, 1)
                dve.wait_ge(spec_step, n + 3)
                dve.wait_ge(zh2_ready, g + 1)
                dve.scalar_tensor_tensor(wide_f[2], wide_f[0], GS, z2[:, bass.ds(g * BT, BT), 0:C],
                                         ALU.mult, ALU.subtract).then_inc(spec_step, 1)

            dve.wait_ge(act_prep, 5)
            dve.wait_ge(pack_ready, NC * T)
            spectrum(0, 0, True)
            spectrum(1, 1, False)
            with dve.Fori(1, G // 2) as q:
                for par in range(2):
                    spectrum(2 * q + par, par, False)

            def rows(ib, k, first):
                n, par = FIN3 * ib, k % 2
                if not (first and k == 0):
                    dve.wait_ge(fin3, n)
                dve.wait_ge(lo3_ready, ib + 1)
                dve.scalar_tensor_tensor(tt[:, :], bank[4 + k][:, 0:C], 1.0 / GS, u[:, 0:C], ALU.mult, ALU.add
                                         ).then_inc(fin3, 1)
                dve.wait_ge(fin3, n + 1)
                dve.wait_ge(xr_loaded[par], 8 * (ib - par) + 16)
                dve.tensor_tensor(tt[:, :], tt[:, :], xt[:, par, :], ALU.add).then_inc(fin3, 1)
                dve.wait_ge(fin3, n + 2)
                dve.bn_stats(st[:, :], tt[:, :]).then_inc(fin3, 1)
                dve.wait_ge(fin3, n + 3)
                passed(dve, "dve")
                dve.bn_aggr(mv[:, :], st[:, :]).then_inc(fin3, 1)
                dve.wait_ge(sd3_ready, ib + 1)
                dve.reciprocal(col[:, 3:4], sd[:, :]).then_inc(fin3, 1)
                dve.wait_ge(fin3, n + 5)
                if not (first and k < 2):
                    dve.wait_ge(out_stored[par], 8 * (ib - par))
                dve.tensor_scalar(x1[:, par, :], tt[:, :], mv[:, 0:1], col[:, 3:4], ALU.subtract, ALU.mult
                                  ).then_inc(fin3, 1)

            for par in range(2):
                dve.wait_ge(x1_stored[par], 16 * (T // 2))
            dve.wait_ge(y_step, YST * T)
            for k in range(RING):
                rows(k, k, True)
            with dve.Fori(1, T // RING) as q:
                for k in range(RING):
                    rows(RING * q + k, k, False)

        @block.tensor
        def _(pe):
            pe.wait_ge(weights_loaded, 48)
            for k in range(KE):
                last = pe.matmul(bank[1][:, 2 * k:2 * k + 2], w1s[:, k * P:(k + 1) * P], w23s[:, :],
                                 start=True, stop=True)
            last.then_inc(v_summed, 1)
            pe.wait_ge(v_ready, 1)
            for s in range(NB):
                pe.wait_ge(in2_loaded[s], 16)
                for t in range(s * BT, (s + 1) * BT):
                    for k in range(KE):
                        last = pe.matmul(bank[0][:, 2 * t:2 * t + 2], in2[:, k, t * P:(t + 1) * P], v23[:, k, :],
                                         start=(k == 0), stop=(k == KE - 1))
            last.then_inc(fcol_summed, 1)
            pe.wait_ge(ident_step, 4)
            pe.wait_ge(ones_ready, 3)
            pe.wait_ge(dve_prep, 1)
            pe.matmul(bank[5][0:T, 0:P], f2[:, :], identf[:, :], start=True, stop=True).then_inc(f2T_turned, 1)
            pe.wait_ge(dve_prep, 2)
            pe.matmul(bank[6][0:1, 0:P], top[:, :], identf[:, :], start=True, stop=True).then_inc(top_turned, 1)
            pe.wait_ge(dve_prep, 4)
            pe.matmul(bank[7][:, 0:1], ones[:, :], top1[:, :], start=True, stop=True).then_inc(top_spread, 1)
            pe.wait_ge(x_loaded, 16)
            for t in range(T):
                last = pe.matmul(bank[2][:, 0:C], inv_n[:, :], x_all[:, t, :], start=(t == 0), stop=(t == T - 1))
            last.then_inc(mean_summed, 1)

            def transposes(ib, b, fresh):
                n = NB * ib + b
                pe.wait_ge(label_ready, n + 1)
                if not (fresh and b < 4):
                    pe.wait_ge(aT_ready, n - 3)
                for k in range(BT):
                    last = pe.transpose(tp[b % 4][:, k * P:(k + 1) * P], label_t[:, b % LB, k * P:(k + 1) * P],
                                        ident[:, :])
                last.then_inc(transposed, 1)

            def products(ib, b, par, fresh, reuse):
                n = NB * ib + b
                pe.wait_ge(masks_ready, n + 1)
                if fresh:
                    pe.wait_ge(zlo_ready, 2 * b + 2)
                if reuse and b == 0:
                    pe.wait_ge(fin, FIN * ib - 2 * FIN + 4)
                for k in range(BT):
                    t = b * BT + k
                    for m, mask in enumerate((m_pos, m_neg)):
                        last = pe.matmul(acc(par, m), mask[:, b % 2, k * P:(k + 1) * P], z[:, t, m, :],
                                         start=(t == 0), stop=(t == T - 1))
                last.then_inc(multiplied, 1)

            def row_block(ib, par, fresh, last, reuse):
                for b in range(NB):
                    if b + 2 < NB:
                        transposes(ib, b + 2, fresh)
                    elif not last:
                        transposes(ib + 1, b + 2 - NB, False)
                    products(ib, b, par, fresh, reuse)

            pe.wait_ge(f2T_ready, 1)
            pe.wait_ge(dve_prep, 22)
            transposes(0, 0, True)
            transposes(0, 1, True)
            row_block(0, 0, True, False, False)
            row_block(1, 1, False, False, False)
            with pe.Fori(1, T // 2 - 1) as q:
                for par in range(2):
                    row_block(2 * q + par, par, False, False, True)
            row_block(T - 2, 0, False, False, True)
            row_block(T - 1, 1, False, True, True)

            def group(g, par, first):
                if first and par == 0:
                    pe.wait_ge(aT_ready, NB * T)
                    pe.wait_ge(y_step, YST * (T - 1))
                if first and par == 1:
                    pe.wait_ge(fin, FIN * T)
                if not first:
                    pe.wait_ge(spec_step, SPEC * g - 2 * SPEC + 1)
                for k in range(NPC):
                    pe.wait_ge(piece_loaded[k % RING], 16 * (NPC // RING) * g + 16 * (k // RING) + 16)
                    if first and par == 0 and k == NPC - 1:
                        pe.wait_ge(y_step, YST * T)
                    passed(pe, "pe")
                    for r in range(PI):
                        it = k * PI + r
                        for jt in range(BT):
                            last = pe.matmul(bank[4 - 4 * par + jt // 2][:, (jt % 2) * 2 * C:(jt % 2 + 1) * 2 * C],
                                             piece[:, k % RING, r, jt * P:(jt + 1) * P], y[:, it, :],
                                             start=(it == 0 and jt % 2 == 0), stop=(it == T - 1),
                                             skip_group_check=True)
                    last.then_inc(piece_used, 1)

            group(0, 0, True)
            group(1, 1, True)
            with pe.Fori(1, G // 2) as q:
                for par in range(2):
                    group(2 * q + par, par, False)

            def sums(k, ts):
                for t in ts:
                    last = pe.matmul(bank[4 + k][:, 0:2 * C], slab[:, k, t * P:(t + 1) * P], z2[:, t, :],
                                     start=(t == 0), stop=(t == T - 1))
                return last

            def rows(ib, k):
                pe.wait_ge(slab_loaded[k], (4 * (ib - k)) + 16)
                pe.wait_ge(fin3, FIN3 * ib - RING * FIN3 + 1)
                passed(pe, "pe")
                sums(k, range(T)).then_inc(rows_done, 1)

            pe.wait_ge(z2_ready, G - 1)
            for k in range(RING):
                pe.wait_ge(slab_loaded[k], 16)
                sums(k, range(T - BT))
            pe.wait_ge(z2_ready, G)
            for k in range(RING):
                sums(k, range(T - BT, T)).then_inc(rows_done, 1)
            with pe.Fori(1, T // RING) as q:
                for k in range(RING):
                    rows(RING * q + k, k)


def kernel(**inputs):
    import numpy as np
    import concourse.bacc as bacc
    from concourse import mybir as mb
    from concourse.bass_utils import run_bass_kernel_spmd as run

    nc = bacc.Bacc("TRN2", target_bir_lowering=False, num_devices=1)
    a = {k: np.asarray(v) for k, v in inputs.items()}
    n = a["x"].shape[0]
    laid_out = {
        "adj": a["adj"],
        "x": a["x"],
        "in2T": a["L0_gnn_inlayer2"].T,
        "W1": a["L0_gnn_W1"],
        "w23": np.stack([a["L0_gnn_w2"], a["L0_gnn_w3"]], axis=1),
        "b23": np.stack([a["L0_gnn_b2"], a["L0_gnn_b3"]]).reshape(2),
        "mass_t": a["L1_gnn_mass"].reshape(n // P, P).T,
        "evals0": a["L1_gnn_evals0"],
        "evals1": a["L1_gnn_evals1"].reshape(P, 1),
        "dt_rows": a["L1_gnn_diffusion_time"],
    }
    arrays, args = {}, []
    for name, v in laid_out.items():
        v = np.ascontiguousarray(v)
        arrays[f"in_{name}"] = v
        args.append(nc.dram_tensor(f"in_{name}", v.shape, mb.dt.from_np(v.dtype), kind="ExternalInput").ap())
    out = nc.dram_tensor("out_0", a["x"].shape, mb.dt.float32, kind="ExternalOutput").ap()
    build(nc, *args, out)
    r = run(nc, [arrays], core_ids=[0])
    return r.results[0]["out_0"]
```

```python
import concourse.bass as bass
from concourse import mybir
from contextlib import ExitStack

P = 128


def build(nc, adj, x, in2T, W1, w32, b32, mass_t, evals0, evals1, dt_rows, out):
    fp32, bf16, fp16 = mybir.dt.float32, mybir.dt.bfloat16, mybir.dt.float16
    fp8, u8, u16 = mybir.dt.float8e4, mybir.dt.uint8, mybir.dt.uint16
    ALU, ACT, AX = mybir.AluOpType, mybir.ActivationFunctionType, mybir.AxisListType

    N, C = x.shape
    EMB2 = in2T.shape[0]
    KE = EMB2 // P
    T = N // P
    BT = 8
    BW = BT * P
    NB = T // BT
    FW = 512
    FC = N // FW
    NC = NB // 2
    LEAD = 3
    LB = 4
    HB = NB // 2
    Z = 2 * (C + 1)
    ZL = C + 1
    LO = 2.0 ** 11
    ZS = 2.0 ** 6
    YS = 2.0 ** 8
    GS = 2.0 ** -2
    EPS = 1e-5
    SLOPE = 0.01
    EDGE = 0x3F80
    EDGE8 = 1.875
    XA = 3 * T // 4
    G = NB
    PI = 8
    NPC = T // PI
    RING = 4

    adjT8 = nc.dram_tensor("adjT8", (T, P, T * P), u8, kind="Internal").ap()
    adj8 = nc.dram_tensor("adj8", (T, P, T * P), u8, kind="Internal").ap()
    adj8_g = adj8.rearrange("t p (g j) -> g t p j", g=G)
    x1_d = nc.dram_tensor("x1_d", (T, P, C), fp32, kind="Internal").ap()
    f_d = nc.dram_tensor("f_d", (2, N), fp32, kind="Internal").ap()
    x_t = x.rearrange("(t p) c -> t p c", p=P)
    out_t = out.rearrange("(t p) c -> t p c", p=P)
    adj_t = adj.rearrange("(t p) j -> t p j", p=P)

    ctx = ExitStack()
    with ctx:
        def sb(name, shape, dt):
            return ctx.enter_context(nc.sbuf_tensor(name, shape, dt))

        def sem(name):
            return ctx.enter_context(nc.semaphore(name))

        f2_region = sb("f2_region", [P, N * 4], u8)
        f2row = f2_region[:, :].bitcast(fp32)
        f_rows = f2row[0:2, :]
        piece_b = f2_region[:, :].rearrange("p (r t j) -> p r t j", r=RING, t=PI)
        piece = f2_region[:, :].bitcast(fp8).rearrange("p (r t j) -> p r t j", r=RING, t=PI)
        z_region = sb("z_region", [P, T * 2 * Z * 2], u8)
        z = z_region[:, :].bitcast(fp16).rearrange("p (t m c) -> p t m c", m=2, c=Z)
        in2 = z_region[:, 0:KE * N * 4].bitcast(fp32).rearrange("p (k n) -> p k n", k=KE)
        z2 = z_region[:, 0:T * 2 * C * 2].bitcast(fp16).rearrange("p (t c) -> p t c", t=T)
        slab_b = z_region[:, N * 4:N * 4 + RING * N].rearrange("p (r j) -> p r j", r=RING)
        slab = z_region[:, N * 4:N * 4 + RING * N].bitcast(fp8).rearrange("p (r j) -> p r j", r=RING)
        y_region = sb("y_region", [P, T * 2 * C * 2], u8)
        y = y_region[:, :].bitcast(fp16).rearrange("p (t c) -> p t c", t=T)
        x_all = y_region[:, :].bitcast(fp32).rearrange("p (t c) -> p t c", t=T)
        stage = sb("stage", [P, NB, BW], fp32)
        adj_hi = stage[:, :, :].bitcast(u16).rearrange("p b (j h) -> p b j h", h=2)[:, :, :, 1]
        wide_f = [stage[:, k, :].rearrange("p (t c) -> p t c", t=BT) for k in range(3)]
        adj_b = stage[:, :, :].rearrange("p b j -> p (b j)").bitcast(u8).rearrange(
            "p (c j h) -> p c j h", c=NC, h=4)[:, :, :, 3]
        zt_region = sb("zt_region", [P, 2 * BT * C * 4], u8)
        zt = zt_region[:, :].bitcast(fp32).rearrange("p (m t c) -> p m t c", m=2, t=BT)
        packed = zt_region[:, 0:N].rearrange("p (h j) -> p h j", h=2)
        label = sb("label", [P, LB, BW], u16)
        label_t = label[:, :, :].bitcast(bf16)
        labT = sb("labT", [P, 2, BW], u16)
        m_pos = sb("m_pos", [P, 2, BW], bf16)
        m_neg = sb("m_neg", [P, 2, BW], bf16)
        aT_half = sb("aT_half", [P, 2, HB * BW], u8)
        ident = sb("ident", [P, P], bf16)
        prep = m_neg[:, :, :].rearrange("p a b -> p (a b)").bitcast(fp32)
        identf, ones, w1s = prep[:, 0:P], prep[0:1, P:2 * P], prep[:, 4 * P:4 * P + EMB2]
        fT = prep[0:T, 2 * P:4 * P].rearrange("t (r p) -> t r p", r=2)
        inv_n = sb("inv_n", [P, P], fp32)
        w32s = sb("w32s", [P, 2], fp32)
        b32s = sb("b32s", [2, 1], fp32)
        v32 = sb("v32", [P, KE, 2], fp32)
        nf1 = sb("nf1", [P, T], fp32)
        tops = sb("tops", [1, FC], fp32)
        top1 = sb("top1", [1, 1], fp32)
        F2 = sb("F2", [P, 1], fp32)
        tmp_a = sb("tmp_a", [P, T], fp32)
        tmp_b = sb("tmp_b", [P, T], fp32)
        row_pos = sb("row_pos", [P, 2, T], fp32)
        row_neg = sb("row_neg", [P, 2, T], fp32)
        f2s = sb("f2s", [P, T], fp32)
        wj = sb("wj", [P, 2, T], fp32)
        mass = sb("mass", [P, T], fp32)
        xmean = sb("xmean", [P, C], fp32)
        eps = sb("eps", [P, 1], fp32)
        ev0 = sb("ev0", [P, T], fp32)
        ev1 = sb("ev1", [P, 1], fp32)
        dts = sb("dts", [P, 2, C], fp32)
        e1 = sb("e1", [P, C], fp32)
        xt = sb("xt", [P, 2, C], fp32)
        u = sb("u", [P, ZL], fp32)
        col = sb("col", [P, 4], fp32)
        tt = sb("tt", [P, C], fp32)
        st = sb("st", [P, 6], fp32)
        mv = sb("mv", [P, 2], fp32)
        sd = sb("sd", [P, 1], fp32)
        x1 = sb("x1", [P, 2, C], fp32)
        ym = sb("ym", [P, C], fp32)

        bank = [ctx.enter_context(nc.psum_tensor(f"bank{k}", [P, 512], fp32)) for k in range(8)]
        tp = [bank[4 + k][:, :].bitcast(bf16) for k in range(4)]
        tp_u16 = [bank[4 + k][:, :].bitcast(u16) for k in range(4)]
        tp_hi8 = [bank[4 + k][:, :].bitcast(fp8).rearrange("p (j h) -> p j h", h=2)[:, :, 1] for k in range(4)]

        f_bank = [bank[k][0:2, :] for k in (0, 2, 3)]

        def acc(ib_par, m):
            return bank[2 * ib_par + m][:, 0:Z]

        weights_loaded, consts_loaded = map(sem, ("weights_loaded", "consts_loaded"))
        x_loaded = [sem(f"x_loaded{k}") for k in range(2)]
        in2_loaded = [sem(f"in2_loaded{k}") for k in range(NB)]
        ident_step, ones_ready = sem("ident_step"), sem("ones_ready")
        v_summed, v_ready, f_summed, f_rows_ready, top_step, top_spread, f_stored, fT_loaded, f_turned = map(
            sem, ("v_summed", "v_ready", "f_summed", "f_rows_ready", "top_step", "top_spread", "f_stored",
                  "fT_loaded", "f_turned"))
        f2row_loaded = [sem(f"f2row_loaded{k}") for k in range(2)]
        mean_summed, mean_ready, dve_prep, act_prep = map(sem, ("mean_summed", "mean_ready", "dve_prep", "act_prep"))
        zt_ready = [sem(f"zt_ready{m}") for m in range(2)]
        zhi_ready, zlo_ready = sem("zhi_ready"), sem("zlo_ready")
        adj_loaded = [sem(f"adj_loaded{k}") for k in range(NC)]
        pack_ready = sem("pack_ready")
        pack_stored = [sem(f"pack_stored{k}") for k in range(2)]
        label_ready, transposed, labT_ready, aT_ready, masks_ready, multiplied = map(sem, (
            "label_ready", "transposed", "labT_ready", "aT_ready", "masks_ready", "multiplied"))
        aT_stored = [sem(f"aT_stored{k}") for k in range(2)]
        xt_loaded = [sem(f"xt_loaded{k}") for k in range(2)]
        x1_stored = [sem(f"x1_stored{k}") for k in range(2)]
        fin, sd_ready, y_step = sem("fin"), sem("sd_ready"), sem("y_step")
        piece_loaded = [sem(f"piece_loaded{k}") for k in range(RING)]
        piece_used = sem("piece_used")
        lo_ready, spec_step, e_arg_ready, e_ready, zh2_ready, z2_ready = map(sem, (
            "lo_ready", "spec_step", "e_arg_ready", "e_ready", "zh2_ready", "z2_ready"))
        slab_loaded = [sem(f"slab_loaded{k}") for k in range(RING)]
        rows_done, lo3_ready, fin3, sd3_ready = map(sem, ("rows_done", "lo3_ready", "fin3", "sd3_ready"))
        xr_loaded = [sem(f"xr_loaded{k}") for k in range(2)]
        out_stored = [sem(f"out_stored{k}") for k in range(2)]

        FIN = 13
        FIN3 = 6
        SPEC = 4
        YST = 3

        block = ctx.enter_context(nc.Block())

        def ab(t, shape):
            return t.to_broadcast(shape)

        waits_passed = {n: sem(f"waits_passed_{n}") for n in ("sp", "pool", "dve", "pe")}

        def passed(eng, name):
            eng.sem_inc(waits_passed[name], 1)

        @block.sync
        def _(sp):
            sp.dma_start(w1s[:, :], W1).then_inc(weights_loaded, 16)
            sp.dma_start(w32s[:, :], w32).then_inc(weights_loaded, 16)
            sp.dma_start(b32s[:, :], b32).then_inc(weights_loaded, 16)
            for s in range(NB):
                sp.dma_start(in2[:, :, s * BW:(s + 1) * BW],
                             in2T[:, s * BW:(s + 1) * BW].rearrange("(k p) n -> p k n", p=P)
                             ).then_inc(in2_loaded[s], 16)

            def load_x(k):
                ts = slice(k * XA, T if k else XA)
                sp.dma_start(x_all[:, ts, :], x_t[ts].rearrange("t p c -> p t c")).then_inc(x_loaded[k], 16)

            load_x(0)

            def load_adj(ib, c):
                sp.dma_start(stage[:, 2 * c:2 * c + 2, :],
                             adj_t[ib, :, 2 * c * BW:(2 * c + 2) * BW].rearrange("p (b j) -> p b j", b=2)
                             ).then_inc(adj_loaded[c], 16)

            def load_f2row(k):
                sp.dma_start(f2row[:, k * HB * BW:(k + 1) * HB * BW],
                             f_d[0, k * HB * BW:(k + 1) * HB * BW].partition_broadcast(P)
                             ).then_inc(f2row_loaded[k], 16)

            sp.wait_ge(f_rows_ready, FC)
            sp.dma_start(f_d, f_rows).then_inc(f_stored, 16)
            load_adj(0, 0)
            sp.wait_ge(f_stored, 16)
            sp.dma_start(fT, f_d.rearrange("r (t p) -> t r p", p=P)).then_inc(fT_loaded, 16)
            sp.wait_ge(top_step, FC)
            load_f2row(0)
            load_adj(0, 1)
            load_x(1)
            load_f2row(1)
            for c in range(2, NC):
                load_adj(0, c)

            def load_xt(ib, par):
                sp.dma_start(xt[:, par, :], x_t[ib]).then_inc(xt_loaded[par], 16)

            def store_x1(ib, par):
                sp.wait_ge(fin, FIN * ib + FIN)
                passed(sp, "sp")
                sp.dma_start(x1_d[ib], x1[:, par, :]).then_inc(x1_stored[par], 16)

            def row_block(ib, par, last, first=False, after=True):
                for c in range(NC):
                    sp.wait_ge(label_ready, NB * ib + 2 * c + 2)
                    passed(sp, "sp")
                    sp.wait_ge(pack_ready, NC * ib + c + 1)
                    passed(sp, "sp")
                    if not last:
                        load_adj(ib + 1, c)
                    if c % 2 == 1:
                        sp.dma_start(adj8[ib, :, c // 2 * HB * BW:(c // 2 + 1) * HB * BW],
                                     aT_half[:, 1, :] if first and c == 1 else packed[:, c // 2, :]
                                     ).then_inc(pack_stored[c // 2], 16)
                    if c == 0 and after:
                        store_x1(ib - 2, par)
                        load_xt(ib, par)

            for par in range(2):
                load_xt(par, par)
            row_block(0, 0, False, True, False)
            row_block(1, 1, False, False, False)
            with sp.Fori(1, T // 2 - 1) as q:
                for par in range(2):
                    row_block(2 * q + par, par, False)
            row_block(T - 2, 0, False)
            row_block(T - 1, 1, True)

            sp.wait_ge(label_ready, NB * T)

            def load_piece(g, k, reuse):
                if reuse:
                    sp.wait_ge(piece_used, NPC * g + k - RING + 1)
                passed(sp, "sp")
                sp.dma_start(piece_b[:, k % RING],
                             adj8_g[g, k * PI:(k + 1) * PI].rearrange("t p j -> p t j")
                             ).then_inc(piece_loaded[k % RING], 16)

            for k in range(NPC):
                if k == NPC - 1:
                    for h in range(2):
                        sp.wait_ge(pack_stored[h], 16 * T)
                elif k == 0:
                    sp.wait_ge(pack_stored[0], 16 * (T - 1))
                load_piece(0, k, k >= RING)
                if k == RING - 1:
                    for par in range(2):
                        store_x1(T - 2 + par, par)
            with sp.Fori(1, G) as g:
                for k in range(NPC):
                    load_piece(g, k, True)

            for h in range(2):
                sp.wait_ge(aT_stored[h], 16 * T)
                sp.wait_ge(x1_stored[h], 16 * (T // 2))
            sp.wait_ge(multiplied, NB * T)

            def out_store(ib, par):
                sp.wait_ge(fin3, FIN3 * ib + FIN3)
                passed(sp, "sp")
                sp.dma_start(out_t[ib], x1[:, par, :]).then_inc(out_stored[par], 16)

            def load_slab(ib, k, first):
                if not first:
                    sp.wait_ge(rows_done, ib - RING + 1)
                passed(sp, "sp")
                sp.dma_start(slab_b[:, k, :], adjT8[ib]).then_inc(slab_loaded[k], 16)

            def load_x1(ib, par, first):
                if not first:
                    sp.wait_ge(fin3, FIN3 * (ib - 2) + 2)
                passed(sp, "sp")
                sp.dma_start(xt[:, par, :], x1_d[ib]).then_inc(xr_loaded[par], 16)

            sp.wait_ge(fin, FIN * T)
            for k in range(RING):
                load_slab(k, k, True)
            for k in range(2):
                load_x1(k, k, True)
            with sp.Fori(0, T // RING - 1) as q:
                for k in range(RING):
                    ib = RING * q + k
                    load_slab(ib + RING, k, False)
                    out_store(ib, k % 2)
                    load_x1(ib + 2, k % 2, False)
            for k in range(RING):
                ib = T - RING + k
                out_store(ib, k % 2)
                if k < 2:
                    load_x1(ib + 2, k % 2, False)
            for par in range(2):
                sp.wait_ge(out_stored[par], 16 * (T // 2))

        @block.gpsimd
        def _(pool):
            pool.memset(ident[:, :], 0.0).then_inc(ident_step, 1)
            pool.memset(identf[:, :], 0.0).then_inc(ident_step, 1)
            pool.memset(inv_n[:, :], 1.0 / N).then_inc(ones_ready, 1)
            pool.memset(ones[:, :], 1.0).then_inc(ones_ready, 1)
            pool.memset(eps[:, :], EPS).then_inc(ones_ready, 1)
            pool.wait_ge(ident_step, 2)
            for m in (ident, identf):
                pool.affine_select(out=m[:, :], in_=m[:, :], compare_op=ALU.not_equal, fill=1.0,
                                   base=0, pattern=[[-1, P]], channel_multiplier=1).then_inc(ident_step, 1)
            pool.dma_start(mass[:, :], mass_t).then_inc(consts_loaded, 16)
            pool.dma_start(ev0[:, :], evals0.partition_broadcast(P)).then_inc(consts_loaded, 16)
            pool.dma_start(ev1[:, :], evals1).then_inc(consts_loaded, 16)
            pool.dma_start(dts[:, :, :], dt_rows.partition_broadcast(P)).then_inc(consts_loaded, 16)

            def pack(ib, c, first):
                pool.wait_ge(adj_loaded[c], 16 * ib + 16)
                if c % 2 == 0 and not first:
                    pool.wait_ge(pack_stored[c // 2], 16 * ib)
                passed(pool, "pool")
                half = aT_half[:, 1, :] if first and c < NC // 2 else packed[:, c // 2, :]
                pool.affine_select(out=half[:, c % 2 * 2 * BW:(c % 2 + 1) * 2 * BW], in_=adj_b[:, c, :],
                                   compare_op=ALU.not_equal, fill=0, base=1, pattern=[[0, 2 * BW]],
                                   channel_multiplier=0).then_inc(pack_ready, 1)

            pool.wait_ge(x_loaded[0], 16)
            pool.wait_ge(dve_prep, 8)
            for h in range(NB):
                if h == XA // BT:
                    pool.wait_ge(x_loaded[1], 16)
                for m in range(2):
                    if h >= 1:
                        pool.wait_ge(zlo_ready, 2 * h + m - 1)
                    pool.tensor_tensor(zt[:, m], x_all[:, h * BT:(h + 1) * BT, :],
                                       wj[:, m, h * BT:(h + 1) * BT].unsqueeze(2).to_broadcast([P, BT, C]),
                                       ALU.mult).then_inc(zt_ready[m], 1)
                if 1 <= h < 3:
                    pack(0, h - 1, True)

            def y_of(ib, par, first=False):
                if not first:
                    pool.wait_ge(y_step, YST * ib)
                pool.wait_ge(fin, FIN * ib + FIN)
                pool.tensor_tensor(ym[:, :], x1[:, par, :], ab(mass[:, bass.ds(ib, 1)], [P, C]), ALU.mult
                                   ).then_inc(y_step, 1)
                pool.wait_ge(y_step, YST * ib + 1)
                pool.tensor_copy(y[:, ib, 0:C], ym[:, :]
                                 ).then_inc(y_step, 1)
                pool.wait_ge(y_step, YST * ib + 2)
                pool.tensor_tensor(y[:, ib, C:2 * C], ym[:, :], y[:, ib, 0:C], ALU.subtract
                                   ).then_inc(y_step, 1)

            pool.wait_ge(zlo_ready, 2 * NB)
            def row_block(ib, par, first=False):
                pack(ib, 0, False)
                pack(ib, 1, False)
                pack(ib, 2, False)
                pack(ib, 3, False)
                if first:
                    pool.wait_ge(mean_ready, 1)
                y_of(ib - 1, 1 - par, first)

            for c in range(NC // 2, NC):
                pack(0, c, True)
            row_block(1, 1, True)
            with pool.Fori(1, T // 2) as q:
                for par in range(2):
                    row_block(2 * q + par, par)
            y_of(T - 1, 1)

        @block.scalar
        def _(act):
            act.wait_ge(dve_prep, 1)
            act.activation(e1[:, :], e1[:, :], ACT.Exp, scale=-1.0).then_inc(act_prep, 1)
            act.wait_ge(dve_prep, 4)
            act.activation(wj[:, 0, :], f2s[:, :], ACT.Exp).then_inc(act_prep, 1)
            act.activation(wj[:, 1, :], f2s[:, :], ACT.Exp, scale=SLOPE).then_inc(act_prep, 1)
            act.wait_ge(dve_prep, 6)
            act.activation(row_pos[:, 0, :], tmp_a[:, :], ACT.Exp, scale=1.0 - SLOPE).then_inc(act_prep, 1)
            act.activation(row_neg[:, 0, :], tmp_b[:, :], ACT.Exp, scale=SLOPE - 1.0).then_inc(act_prep, 1)

            def split_high(h, m):
                act.wait_ge(zt_ready[m], h + 1)
                act.activation(z[:, h * BT:(h + 1) * BT, m, 0:C], zt[:, m], ACT.Copy, scale=1.0 / LO
                               ).then_inc(zhi_ready, 1)

            def bank_out(ib, b, first):
                n = NB * ib + b
                act.wait_ge(transposed, n + 1)
                if not (first and b < 2):
                    act.wait_ge(masks_ready, n - 1)
                if first and b == HB:
                    act.wait_ge(pack_stored[0], 16)
                if not first and b % HB == 0:
                    act.wait_ge(aT_stored[b // HB], 16 * ib)
                act.activation(labT[:, b % 2, :], tp_u16[b % 4], ACT.Copy).then_inc(labT_ready, 1)
                dst = aT_half[:, b // HB, (b % HB) * BW:(b % HB + 1) * BW].bitcast(fp8)
                act.activation(dst, tp_hi8[b % 4], ACT.Copy, scale=1.0 / EDGE8, saturate=False
                               ).then_inc(aT_ready, 1)

            def store_aT(ib, h):
                act.wait_ge(aT_ready, NB * ib + HB * (h + 1))
                act.dma_start(adjT8[ib, :, h * HB * BW:(h + 1) * HB * BW], aT_half[:, h, :]
                              ).then_inc(aT_stored[h], 16)

            def deviation(ib):
                act.wait_ge(fin, FIN * ib + 11)
                act.activation(sd[:, :], mv[:, 1:2], ACT.Sqrt, bias=eps[:, :]).then_inc(sd_ready, 1)

            def row_block(ib, first):
                for b in range(NB):
                    bank_out(ib, b, first)
                    if b == 0 and not first:
                        store_aT(ib - 1, 1)
                    if b == HB:
                        store_aT(ib, 0)

            for h in range(NB):
                for m in range(2):
                    split_high(h, m)
                if h >= 1:
                    bank_out(0, h - 1, True)
                if h == HB + 1:
                    store_aT(0, 0)
            bank_out(0, NB - 1, True)
            act.wait_ge(ones_ready, 3)
            row_block(1, False)
            with act.Fori(1, T // 2) as q:
                for par in range(2):
                    deviation(2 * q + par - 2)
                    row_block(2 * q + par, False)
            store_aT(T - 1, 1)
            deviation(T - 2)
            deviation(T - 1)

            def group(g, par, first):
                act.wait_ge(piece_used, NPC * g + NPC)
                if not first:
                    act.wait_ge(spec_step, SPEC * g)
                for k in range(4):
                    act.activation(wide_f[0][:, 2 * k:2 * k + 2, :],
                                   bank[4 - 4 * par + k][:, :].rearrange("p (t c) -> p t c", t=2)[:, :, C:2 * C],
                                   ACT.Copy, scale=1.0 / (YS * EDGE8)).then_inc(lo_ready, 1)
                act.wait_ge(e_arg_ready, g + 1)
                act.activation(wide_f[1], wide_f[1], ACT.Exp, scale=-1.0).then_inc(e_ready, 1)
                act.wait_ge(spec_step, SPEC * g + 3)
                act.activation(z2[:, bass.ds(g * BT, BT), 0:C], wide_f[0], ACT.Copy, scale=GS
                               ).then_inc(zh2_ready, 1)
                act.wait_ge(spec_step, SPEC * g + 4)
                act.activation(z2[:, bass.ds(g * BT, BT), C:2 * C], wide_f[2], ACT.Copy, scale=LO
                               ).then_inc(z2_ready, 1)

            for par in range(2):
                group(par, par, par == 0)
            with act.Fori(1, G // 2) as q:
                for par in range(2):
                    group(2 * q + par, par, False)

            def finish(ib, k):
                act.wait_ge(rows_done, ib + 1)
                act.activation(u[:, 0:C], bank[4 + k][:, C:2 * C], ACT.Copy, scale=1.0 / (LO * GS)
                               ).then_inc(lo3_ready, 1)
                act.wait_ge(fin3, FIN3 * ib + 4)
                act.activation(sd[:, :], mv[:, 1:2], ACT.Sqrt, bias=eps[:, :]).then_inc(sd3_ready, 1)

            for k in range(RING):
                finish(k, k)
            with act.Fori(1, T // RING) as q:
                for k in range(RING):
                    finish(RING * q + k, k)

        @block.vector
        def _(dve):
            dve.wait_ge(v_summed, 1)
            dve.tensor_copy(v32[:, :, :], bank[1][:, 0:2 * KE].rearrange("p (k w) -> p k w", k=KE)
                            ).then_inc(v_ready, 1)
            dve.wait_ge(weights_loaded, 48)

            def chunk_top(s):
                dve.wait_ge(f_rows_ready, s + 1)
                dve.reduce_max(tops[:, s:s + 1], f_rows[0:1, s * FW:(s + 1) * FW], axis=AX.X).then_inc(top_step, 1)

            for s in range(FC):
                if s == FC - 3:
                    dve.wait_ge(consts_loaded, 64)
                    dve.tensor_scalar(e1[:, :], dts[:, 1, :], ev1[:, :], None, ALU.mult).then_inc(dve_prep, 1)
                    dve.tensor_scalar(mass[:, :], mass[:, :], YS, None, ALU.mult).then_inc(dve_prep, 1)
                dve.wait_ge(f_summed, s + 1)
                dve.tensor_scalar(f_rows[:, s * FW:(s + 1) * FW], f_bank[s % 3], b32s[:, :], None, ALU.add
                                  ).then_inc(f_rows_ready, 1)
                if s >= 1:
                    chunk_top(s - 1)
            chunk_top(FC - 1)
            dve.wait_ge(top_step, FC)
            dve.reduce_max(top1[:, :], tops[:, :], axis=AX.X).then_inc(top_step, 1)
            dve.wait_ge(top_spread, 1)
            dve.tensor_copy(F2[:, :], bank[1][:, 2 * KE:2 * KE + 1]).then_inc(dve_prep, 1)
            dve.wait_ge(dve_prep, 3)
            dve.wait_ge(f_turned, 1)
            f2, f1 = bank[3][:, 0:T], bank[3][:, T:2 * T]
            dve.tensor_scalar(f2s[:, :], f2, F2[:, :], None, ALU.subtract).then_inc(dve_prep, 1)
            dve.tensor_scalar(tmp_a[:, :], f1, F2[:, :], 0.0, ALU.add, ALU.min).then_inc(dve_prep, 1)
            dve.tensor_scalar(tmp_b[:, :], f1, F2[:, :], 0.0, ALU.add, ALU.max).then_inc(dve_prep, 1)
            dve.tensor_scalar(nf1[:, :], f1, -1.0, None, ALU.mult).then_inc(dve_prep, 1)

            dve.wait_ge(act_prep, 3)
            dve.tensor_scalar(wj[:, :, :], wj[:, :, :], ZS * LO, None, ALU.mult).then_inc(dve_prep, 1)
            dve.wait_ge(dve_prep, 8)
            for m in range(2):
                dve.tensor_scalar(z[:, :, m, C], wj[:, m, :], 1.0 / LO, None, ALU.mult).then_inc(dve_prep, 1)
            dve.wait_ge(dve_prep, 10)
            for m in range(2):
                dve.scalar_tensor_tensor(z[:, :, m, C + ZL], z[:, :, m, C], -LO, wj[:, m, :], ALU.mult, ALU.add
                                         ).then_inc(dve_prep, 1)
            dve.wait_ge(act_prep, 5)
            for r in (row_pos, row_neg):
                dve.tensor_scalar(r[:, 1, :], r[:, 0, :], 1.0 / (ZS * LO), None, ALU.mult).then_inc(dve_prep, 1)
            dve.wait_ge(dve_prep, 14)
            for r in (row_pos, row_neg):
                dve.tensor_scalar(r[:, 0, :], r[:, 0, :], 1.0 / ZS, None, ALU.mult).then_inc(dve_prep, 1)

            def table_low(h, m):
                dve.wait_ge(zhi_ready, 2 * h + m + 1)
                dve.scalar_tensor_tensor(z[:, h * BT:(h + 1) * BT, m, ZL:ZL + C],
                                         z[:, h * BT:(h + 1) * BT, m, 0:C], -LO, zt[:, m], ALU.mult, ALU.add
                                         ).then_inc(zlo_ready, 1)

            def make_label(ib, b, fresh):
                if b % 2 == 0:
                    dve.wait_ge(adj_loaded[b // 2], 16 * ib + 16)
                dve.scalar_tensor_tensor(label[:, b % LB, :], f2row[:, b * BW:(b + 1) * BW], nf1[:, bass.ds(ib, 1)],
                                         adj_hi[:, b, :], ALU.is_gt, ALU.add).then_inc(label_ready, 1)

            def masks(ib, b, fresh):
                n = NB * ib + b
                dve.wait_ge(labT_ready, n + 1)
                if not (fresh and b < 2):
                    dve.wait_ge(multiplied, n - 1)
                dve.tensor_scalar(m_pos[:, b % 2, :], labT[:, b % 2, :], float(EDGE + 1), None, ALU.is_equal)
                dve.tensor_scalar(m_neg[:, b % 2, :], labT[:, b % 2, :], float(EDGE), None, ALU.is_equal
                                  ).then_inc(masks_ready, 1)

            def finish(ib, par, step, reuse):
                n = FIN * ib
                pos, neg = acc(par, 0), acc(par, 1)
                one = bass.ds(ib, 1)
                if step == 0:
                    dve.wait_ge(multiplied, NB * ib + NB)
                    dve.tensor_scalar(u[:, :], pos[:, 0:ZL], row_pos[:, 0, one], None, ALU.mult).then_inc(fin, 1)
                elif step == 1:
                    dve.wait_ge(fin, n + 1)
                    dve.scalar_tensor_tensor(u[:, :], pos[:, ZL:Z], row_pos[:, 1, one], u[:, :], ALU.mult, ALU.add
                                             ).then_inc(fin, 1)
                elif step == 2:
                    dve.wait_ge(fin, n + 2)
                    dve.scalar_tensor_tensor(u[:, :], neg[:, 0:ZL], row_neg[:, 0, one], u[:, :], ALU.mult, ALU.add
                                             ).then_inc(fin, 1)
                elif step == 3:
                    dve.wait_ge(fin, n + 3)
                    dve.scalar_tensor_tensor(u[:, :], neg[:, ZL:Z], row_neg[:, 1, one], u[:, :], ALU.mult, ALU.add
                                             ).then_inc(fin, 1)
                elif step == 4:
                    dve.wait_ge(fin, n + 4)
                    dve.tensor_scalar(col[:, 0:1], u[:, C:ZL], 0.0, None, ALU.is_le).then_inc(fin, 1)
                elif step == 5:
                    dve.wait_ge(fin, n + 5)
                    dve.tensor_tensor(col[:, 1:2], u[:, C:ZL], col[:, 0:1], ALU.add).then_inc(fin, 1)
                elif step == 6:
                    dve.wait_ge(fin, n + 6)
                    dve.reciprocal(col[:, 2:3], col[:, 1:2]).then_inc(fin, 1)
                elif step == 7:
                    dve.scalar_tensor_tensor(tt[:, :], xmean[:, :], col[:, 0:1], u[:, 0:C], ALU.mult, ALU.add
                                             ).then_inc(fin, 1)
                elif step == 8:
                    dve.wait_ge(fin, n + 8)
                    dve.wait_ge(xt_loaded[par], 8 * (ib - par) + 16)
                    dve.scalar_tensor_tensor(tt[:, :], tt[:, :], col[:, 2:3], xt[:, par, :], ALU.mult, ALU.add
                                             ).then_inc(fin, 1)
                elif step == 9:
                    dve.wait_ge(fin, n + 9)
                    dve.bn_stats(st[:, :], tt[:, :]).then_inc(fin, 1)
                elif step == 10:
                    dve.wait_ge(fin, n + 10)
                    passed(dve, "dve")
                    dve.bn_aggr(mv[:, :], st[:, :]).then_inc(fin, 1)
                elif step == 11:
                    dve.wait_ge(sd_ready, ib + 1)
                    dve.reciprocal(col[:, 3:4], sd[:, :]).then_inc(fin, 1)
                else:
                    dve.wait_ge(fin, n + 12)
                    if reuse:
                        dve.wait_ge(x1_stored[par], 8 * (ib - par))
                        dve.wait_ge(y_step, YST * ib - 2 * YST + 1)
                    dve.tensor_scalar(x1[:, par, :], tt[:, :], mv[:, 0:1], col[:, 3:4], ALU.subtract, ALU.mult
                                      ).then_inc(fin, 1)

            AFTER_MASKS = ((), (0,), (2,), (4,), (6, 7), (9,), (), ())
            AFTER_LABEL = ((), (1,), (3,), (5,), (8,), (10,), (), (11, 12))

            def row_block(ib, par, last, reuse):
                for b in range(NB):
                    masks(ib, b, False)
                    for step in AFTER_MASKS[b]:
                        finish(ib - 1, 1 - par, step, reuse)
                    if b + LEAD < NB:
                        make_label(ib, b + LEAD, False)
                    elif not last:
                        make_label(ib + 1, b + LEAD - NB, False)
                    for step in AFTER_LABEL[b]:
                        finish(ib - 1, 1 - par, step, reuse)

            for h in range(NB):
                table_low(h, 0)
                table_low(h, 1)
                if h == 0:
                    dve.wait_ge(f2row_loaded[0], 16)
                    make_label(0, 0, True)
                if h + 1 < NB:
                    if h + 1 == HB:
                        dve.wait_ge(f2row_loaded[1], 16)
                    make_label(0, h + 1, True)
                if h >= 1:
                    masks(0, h - 1, True)
            masks(0, NB - 1, True)
            make_label(1, 0, False)
            dve.wait_ge(mean_summed, 1)
            dve.tensor_copy(xmean[:, :], bank[2][:, 0:C]).then_inc(mean_ready, 1)
            for b in range(1, LEAD):
                make_label(1, b, False)
            row_block(1, 1, False, False)
            row_block(2, 0, False, False)
            row_block(3, 1, False, True)
            with dve.Fori(2, T // 2 - 1) as q:
                for par in range(2):
                    row_block(2 * q + par, par, False, True)
            row_block(T - 2, 0, False, True)
            row_block(T - 1, 1, True, True)
            for step in range(FIN):
                finish(T - 1, 1, step, True)

            def spectrum(g, par, first):
                n = SPEC * g
                if not first:
                    dve.wait_ge(z2_ready, g)
                dve.tensor_tensor(wide_f[1], dts[:, 0, :].unsqueeze(1).to_broadcast([P, BT, C]),
                                  ev0[:, bass.ds(g * BT, BT)].unsqueeze(2).to_broadcast([P, BT, C]), ALU.mult
                                  ).then_inc(e_arg_ready, 1)
                for k in range(4):
                    dve.wait_ge(lo_ready, 4 * g + k + 1)
                    last = dve.scalar_tensor_tensor(
                        wide_f[0][:, 2 * k:2 * k + 2, :],
                        bank[4 - 4 * par + k][:, :].rearrange("p (t c) -> p t c", t=2)[:, :, 0:C],
                        1.0 / (YS * EDGE8),
                        wide_f[0][:, 2 * k:2 * k + 2, :], ALU.mult, ALU.add)
                last.then_inc(spec_step, 1)
                dve.wait_ge(spec_step, n + 1)
                dve.tensor_tensor(wide_f[0], wide_f[0], e1[:, :].unsqueeze(1).to_broadcast([P, BT, C]), ALU.mult
                                  ).then_inc(spec_step, 1)
                dve.wait_ge(spec_step, n + 2)
                dve.wait_ge(e_ready, g + 1)
                dve.tensor_tensor(wide_f[0], wide_f[0], wide_f[1], ALU.mult).then_inc(spec_step, 1)
                dve.wait_ge(spec_step, n + 3)
                dve.wait_ge(zh2_ready, g + 1)
                dve.scalar_tensor_tensor(wide_f[2], wide_f[0], GS, z2[:, bass.ds(g * BT, BT), 0:C],
                                         ALU.mult, ALU.subtract).then_inc(spec_step, 1)

            dve.wait_ge(act_prep, 5)
            dve.wait_ge(pack_ready, NC * T)
            spectrum(0, 0, True)
            spectrum(1, 1, False)
            with dve.Fori(1, G // 2) as q:
                for par in range(2):
                    spectrum(2 * q + par, par, False)

            def rows(ib, k, first):
                n, par = FIN3 * ib, k % 2
                if not (first and k == 0):
                    dve.wait_ge(fin3, n)
                dve.wait_ge(lo3_ready, ib + 1)
                dve.scalar_tensor_tensor(tt[:, :], bank[4 + k][:, 0:C], 1.0 / GS, u[:, 0:C], ALU.mult, ALU.add
                                         ).then_inc(fin3, 1)
                dve.wait_ge(fin3, n + 1)
                dve.wait_ge(xr_loaded[par], 8 * (ib - par) + 16)
                dve.tensor_tensor(tt[:, :], tt[:, :], xt[:, par, :], ALU.add).then_inc(fin3, 1)
                dve.wait_ge(fin3, n + 2)
                dve.bn_stats(st[:, :], tt[:, :]).then_inc(fin3, 1)
                dve.wait_ge(fin3, n + 3)
                passed(dve, "dve")
                dve.bn_aggr(mv[:, :], st[:, :]).then_inc(fin3, 1)
                dve.wait_ge(sd3_ready, ib + 1)
                dve.reciprocal(col[:, 3:4], sd[:, :]).then_inc(fin3, 1)
                dve.wait_ge(fin3, n + 5)
                if not (first and k < 2):
                    dve.wait_ge(out_stored[par], 8 * (ib - par))
                dve.tensor_scalar(x1[:, par, :], tt[:, :], mv[:, 0:1], col[:, 3:4], ALU.subtract, ALU.mult
                                  ).then_inc(fin3, 1)

            for par in range(2):
                dve.wait_ge(x1_stored[par], 16 * (T // 2))
            dve.wait_ge(y_step, YST * T)
            for k in range(RING):
                rows(k, k, True)
            with dve.Fori(1, T // RING) as q:
                for k in range(RING):
                    rows(RING * q + k, k, False)

        @block.tensor
        def _(pe):
            pe.wait_ge(weights_loaded, 48)
            for k in range(KE):
                last = pe.matmul(bank[1][:, 2 * k:2 * k + 2], w1s[:, k * P:(k + 1) * P], w32s[:, :],
                                 start=True, stop=True)
            last.then_inc(v_summed, 1)
            pe.wait_ge(v_ready, 1)
            for s in range(FC):
                pe.wait_ge(in2_loaded[s * FW // BW], 16)
                if s >= len(f_bank):
                    pe.wait_ge(f_rows_ready, s - 2)
                for k in range(KE):
                    last = pe.matmul(f_bank[s % 3], v32[:, k, :], in2[:, k, s * FW:(s + 1) * FW],
                                     start=(k == 0), stop=(k == KE - 1))
                last.then_inc(f_summed, 1)
            pe.wait_ge(ident_step, 4)
            pe.wait_ge(ones_ready, 3)
            pe.wait_ge(top_step, FC + 1)
            pe.matmul(bank[1][:, 2 * KE:2 * KE + 1], ones[:, :], top1[:, :], start=True, stop=True
                      ).then_inc(top_spread, 1)

            pe.wait_ge(fT_loaded, 16)
            for w in range(2):
                last = pe.matmul(bank[3][:, w * T:(w + 1) * T], fT[:, w, :], identf[0:T, 0:T], start=True, stop=True)
            last.then_inc(f_turned, 1)

            def mean(ts):
                for t in ts:
                    last = pe.matmul(bank[2][:, 0:C], inv_n[:, :], x_all[:, t, :], start=(t == 0), stop=(t == T - 1))
                return last

            def transposes(ib, b, fresh):
                n = NB * ib + b
                pe.wait_ge(label_ready, n + 1)
                if not (fresh and b < 4):
                    pe.wait_ge(aT_ready, n - 3)
                for k in range(BT):
                    last = pe.transpose(tp[b % 4][:, k * P:(k + 1) * P], label_t[:, b % LB, k * P:(k + 1) * P],
                                        ident[:, :])
                last.then_inc(transposed, 1)

            def products(ib, b, par, fresh, reuse):
                n = NB * ib + b
                pe.wait_ge(masks_ready, n + 1)
                if fresh:
                    pe.wait_ge(zlo_ready, 2 * b + 2)
                if reuse and b == 0:
                    pe.wait_ge(fin, FIN * ib - 2 * FIN + 4)
                for k in range(BT):
                    t = b * BT + k
                    for m, mask in enumerate((m_pos, m_neg)):
                        last = pe.matmul(acc(par, m), mask[:, b % 2, k * P:(k + 1) * P], z[:, t, m, :],
                                         start=(t == 0), stop=(t == T - 1))
                last.then_inc(multiplied, 1)

            def row_block(ib, par, last, reuse):
                for b in range(NB):
                    if b + 2 < NB:
                        transposes(ib, b + 2, False)
                    elif not last:
                        transposes(ib + 1, b + 2 - NB, False)
                    products(ib, b, par, False, reuse)

            pe.wait_ge(x_loaded[0], 16)
            MB = 3
            mean(range(T - MB * NB))
            transposes(0, 0, True)
            transposes(0, 1, True)
            for b in range(NB):
                if b == 2:
                    pe.wait_ge(x_loaded[1], 16)
                last = mean(range(T - MB * (NB - b), T - MB * (NB - b - 1)))
                if b == NB - 1:
                    last.then_inc(mean_summed, 1)
                if b + 2 < NB:
                    transposes(0, b + 2, True)
                products(0, b, 0, True, False)
            transposes(1, 0, False)
            transposes(1, 1, False)
            row_block(1, 1, False, False)
            with pe.Fori(1, T // 2 - 1) as q:
                for par in range(2):
                    row_block(2 * q + par, par, False, True)
            row_block(T - 2, 0, False, True)
            row_block(T - 1, 1, True, True)

            def group(g, par, first):
                if first and par == 0:
                    pe.wait_ge(aT_ready, NB * T)
                    pe.wait_ge(y_step, YST * (T - 1))
                if first and par == 1:
                    pe.wait_ge(fin, FIN * T)
                if not first:
                    pe.wait_ge(spec_step, SPEC * g - 2 * SPEC + 1)
                for k in range(NPC):
                    pe.wait_ge(piece_loaded[k % RING], 16 * (NPC // RING) * g + 16 * (k // RING) + 16)
                    if first and par == 0 and k == NPC - 1:
                        pe.wait_ge(y_step, YST * T)
                    passed(pe, "pe")
                    for r in range(PI):
                        it = k * PI + r
                        for jt in range(BT):
                            last = pe.matmul(bank[4 - 4 * par + jt // 2][:, (jt % 2) * 2 * C:(jt % 2 + 1) * 2 * C],
                                             piece[:, k % RING, r, jt * P:(jt + 1) * P], y[:, it, :],
                                             start=(it == 0 and jt % 2 == 0), stop=(it == T - 1),
                                             skip_group_check=True)
                    last.then_inc(piece_used, 1)

            group(0, 0, True)
            group(1, 1, True)
            with pe.Fori(1, G // 2) as q:
                for par in range(2):
                    group(2 * q + par, par, False)

            def sums(k, ts):
                for t in ts:
                    last = pe.matmul(bank[4 + k][:, 0:2 * C], slab[:, k, t * P:(t + 1) * P], z2[:, t, :],
                                     start=(t == 0), stop=(t == T - 1))
                return last

            def rows(ib, k):
                pe.wait_ge(slab_loaded[k], (4 * (ib - k)) + 16)
                pe.wait_ge(fin3, FIN3 * ib - RING * FIN3 + 1)
                passed(pe, "pe")
                sums(k, range(T)).then_inc(rows_done, 1)

            pe.wait_ge(z2_ready, G - 1)
            for k in range(2):
                pe.wait_ge(slab_loaded[k], 16)
                sums(k, range(T - BT))
            pe.wait_ge(z2_ready, G)
            for k in range(2):
                sums(k, range(T - BT, T)).then_inc(rows_done, 1)
            for k in range(2, RING):
                pe.wait_ge(slab_loaded[k], 16)
                sums(k, range(T)).then_inc(rows_done, 1)
            with pe.Fori(1, T // RING) as q:
                for k in range(RING):
                    rows(RING * q + k, k)


def kernel(**inputs):
    import numpy as np
    import concourse.bacc as bacc
    from concourse import mybir as mb
    from concourse.bass_utils import run_bass_kernel_spmd as run

    nc = bacc.Bacc("TRN2", target_bir_lowering=False, num_devices=1)
    a = {k: np.asarray(v) for k, v in inputs.items()}
    n = a["x"].shape[0]
    laid_out = {
        "adj": a["adj"],
        "x": a["x"],
        "in2T": a["L0_gnn_inlayer2"].T,
        "W1": a["L0_gnn_W1"],
        "w32": np.stack([a["L0_gnn_w3"], a["L0_gnn_w2"]], axis=1),
        "b32": np.stack([a["L0_gnn_b3"], a["L0_gnn_b2"]]).reshape(2, 1),
        "mass_t": a["L1_gnn_mass"].reshape(n // P, P).T,
        "evals0": a["L1_gnn_evals0"],
        "evals1": a["L1_gnn_evals1"].reshape(P, 1),
        "dt_rows": a["L1_gnn_diffusion_time"],
    }
    arrays, args = {}, []
    for name, v in laid_out.items():
        v = np.ascontiguousarray(v)
        arrays[f"in_{name}"] = v
        args.append(nc.dram_tensor(f"in_{name}", v.shape, mb.dt.from_np(v.dtype), kind="ExternalInput").ap())
    out = nc.dram_tensor("out_0", a["x"].shape, mb.dt.float32, kind="ExternalOutput").ap()
    build(nc, *args, out)
    r = run(nc, [arrays], core_ids=[0])
    return r.results[0]["out_0"]
```
